# Optimizing a Trainium2 kernel written in Bass

```python
import numpy as np
import jax
import jax.numpy as jnp

def _softmax(x, axis=-1):
    return jax.nn.softmax(x, axis=axis)
def _gelu(x):
    return jax.nn.gelu(x, approximate=True)
def _silu(x):
    return jax.nn.silu(x)
def _sigmoid(x):
    return jax.nn.sigmoid(x)
def _layernorm(x, axis=-1, eps=1e-5):
    m = jnp.mean(x, axis=axis, keepdims=True)
    v = jnp.var(x, axis=axis, keepdims=True)
    return (x - m) / jnp.sqrt(v + eps)
def _scatter_add(tgt, idx, src, axis=0):
    return tgt.at[idx].add(src)
def _segment_sum(src, seg, n):
    return jax.ops.segment_sum(src, seg, n)

kernel_name = 'mk_conv_preact_d2_conv_nchw256_8bf67e'

def setup_inputs(seed: int = 0):
    np.random.seed(seed)
    _w = jnp.asarray
    def _rec_inputs():
        import jax
        import jax.numpy as jnp
        _gk = jax.random.key(seed)
        x = 7.22e-05 + 1 * jax.random.normal(jax.random.fold_in(_gk, 1), (8, 256, 64, 64), jnp.float32)
        return x
    x = _rec_inputs()
    def _L0_conv_setup():
        import jax, jax.numpy as jnp
        import numpy as np
        B, C, H, W = (8, 256, 64, 64)
        OUT_C = 256
        K = 3
        DG = 1
        CPG = C // DG
        KK = K * K

        def _sample_group(img, py, px):
            Hh, Ww = (img.shape[1], img.shape[2])
            flat = img.reshape(img.shape[0], Hh * Ww)
            y0 = jnp.floor(py)
            x0 = jnp.floor(px)
            wy = py - y0
            wx = px - x0

            def gather(yi, xi):
                valid = ((yi >= 0) & (yi < Hh) & (xi >= 0) & (xi < Ww)).astype(img.dtype)
                idx = (jnp.clip(yi, 0, Hh - 1) * Ww + jnp.clip(xi, 0, Ww - 1)).astype(jnp.int32)
                v = jnp.take(flat, idx.reshape(-1), axis=1).reshape(img.shape[0], *yi.shape)
                return v * valid
            out = gather(y0, x0) * ((1.0 - wy) * (1.0 - wx)) + gather(y0, x0 + 1.0) * ((1.0 - wy) * wx) + gather(y0 + 1.0, x0) * (wy * (1.0 - wx)) + gather(y0 + 1.0, x0 + 1.0) * (wy * wx)
            return jnp.transpose(out, (1, 0, 2, 3))

        def _forward(x, w_off, b_off, w_conv):
            b = x.shape[0]
            pad = K // 2
            out = jax.lax.conv_general_dilated(x, w_off, window_strides=(1, 1), padding=[(pad, pad), (pad, pad)], dimension_numbers=('NCHW', 'OIHW', 'NCHW')) + b_off[None, :, None, None]
            o1, o2, m = jnp.split(out, 3, axis=1)
            dy = o1.reshape(b, DG, KK, H, W)
            dx = o2.reshape(b, DG, KK, H, W)
            mask = jax.nn.sigmoid(m).reshape(b, DG, KK, 1, H, W)
            ys = jnp.arange(H, dtype=x.dtype)[None, None, None, :, None]
            xs = jnp.arange(W, dtype=x.dtype)[None, None, None, None, :]
            py = ys + dy
            px = xs + dx
            xg = x.reshape(b, DG, CPG, H, W)
            sampled = jax.vmap(jax.vmap(_sample_group))(xg, py, px)
            y = sampled * mask
            y = y.reshape(b, C * KK, H, W)
            return jnp.einsum('bkhw,ok->bohw', y, w_conv)
        key = jax.random.key(seed)
        k1, k2, k3 = jax.random.split(key, 3)
        x = jax.random.normal(k1, (B, C, H, W), jnp.float32)
        w_off = jax.random.normal(k2, (DG * 3 * KK, C, K, K), jnp.float32) * 0.01
        b_off = jnp.zeros((DG * 3 * KK,), jnp.float32)
        w_conv = jax.random.normal(k3, (OUT_C, C * KK), jnp.float32) / np.sqrt(C * KK).astype(np.float32)
        return {'x': x, 'w_off': w_off, 'b_off': b_off, 'w_conv': w_conv}
    _L0_conv_all = _L0_conv_setup()
    _L0_conv_in = {k: v for k, v in _L0_conv_all.items() if k in ('w_off', 'b_off', 'w_conv', )}
    del _L0_conv_all

    def _L1_conv_setup():
        import jax, jax.numpy as jnp
        import numpy as np
        EPS = 1e-12

        def _rms_norm(x, g):
            c = x.shape[1]
            n = jnp.maximum(jnp.linalg.norm(x, axis=1, keepdims=True), EPS)
            return x / n * g * c ** 0.5
        key = jax.random.key(seed)
        ks = jax.random.split(key, 5)
        b, dim, H, W = (32, 256, 64, 64)
        heads, dim_head, num_mem = (4, 32, 4)
        hidden = heads * dim_head
        return {'x': jax.random.normal(ks[0], (b, dim, H, W), dtype=jnp.float32), 'g1': jnp.ones((1, dim, 1, 1), dtype=jnp.float32), 'mem_kv': jax.random.normal(ks[1], (2, heads, dim_head, num_mem), dtype=jnp.float32), 'w_qkv': jax.random.normal(ks[2], (3 * hidden, dim), dtype=jnp.float32) * (1.0 / np.sqrt(dim)), 'w_out': jax.random.normal(ks[3], (dim, hidden), dtype=jnp.float32) * (1.0 / np.sqrt(hidden)), 'b_out': jnp.zeros((dim,), dtype=jnp.float32), 'g2': jnp.ones((1, dim, 1, 1), dtype=jnp.float32)}
    _L1_conv_all = _L1_conv_setup()
    _L1_conv_in = {k: v for k, v in _L1_conv_all.items() if k in ('g1', 'mem_kv', 'w_qkv', 'w_out', 'b_out', 'g2', )}
    del _L1_conv_all

    return {
        "x": x,
        "L0_conv_w_off": _L0_conv_in["w_off"],
        "L0_conv_b_off": _L0_conv_in["b_off"],
        "L0_conv_w_conv": _L0_conv_in["w_conv"],
        "L1_conv_g1": _L1_conv_in["g1"],
        "L1_conv_mem_kv": _L1_conv_in["mem_kv"],
        "L1_conv_w_qkv": _L1_conv_in["w_qkv"],
        "L1_conv_w_out": _L1_conv_in["w_out"],
        "L1_conv_b_out": _L1_conv_in["b_out"],
        "L1_conv_g2": _L1_conv_in["g2"],
    }

def reference(x, L0_conv_w_off, L0_conv_b_off, L0_conv_w_conv, L1_conv_g1, L1_conv_mem_kv, L1_conv_w_qkv, L1_conv_w_out, L1_conv_b_out, L1_conv_g2):
    import jax
    import jax.numpy as jnp
    def _L0_conv_ref(x, w_off, b_off, w_conv):
        import jax, jax.numpy as jnp
        import numpy as np
        B, C, H, W = (8, 256, 64, 64)
        OUT_C = 256
        K = 3
        DG = 1
        CPG = C // DG
        KK = K * K

        def _sample_group(img, py, px):
            Hh, Ww = (img.shape[1], img.shape[2])
            flat = img.reshape(img.shape[0], Hh * Ww)
            y0 = jnp.floor(py)
            x0 = jnp.floor(px)
            wy = py - y0
            wx = px - x0

            def gather(yi, xi):
                valid = ((yi >= 0) & (yi < Hh) & (xi >= 0) & (xi < Ww)).astype(img.dtype)
                idx = (jnp.clip(yi, 0, Hh - 1) * Ww + jnp.clip(xi, 0, Ww - 1)).astype(jnp.int32)
                v = jnp.take(flat, idx.reshape(-1), axis=1).reshape(img.shape[0], *yi.shape)
                return v * valid
            out = gather(y0, x0) * ((1.0 - wy) * (1.0 - wx)) + gather(y0, x0 + 1.0) * ((1.0 - wy) * wx) + gather(y0 + 1.0, x0) * (wy * (1.0 - wx)) + gather(y0 + 1.0, x0 + 1.0) * (wy * wx)
            return jnp.transpose(out, (1, 0, 2, 3))

        def _forward(x, w_off, b_off, w_conv):
            b = x.shape[0]
            pad = K // 2
            out = jax.lax.conv_general_dilated(x, w_off, window_strides=(1, 1), padding=[(pad, pad), (pad, pad)], dimension_numbers=('NCHW', 'OIHW', 'NCHW')) + b_off[None, :, None, None]
            o1, o2, m = jnp.split(out, 3, axis=1)
            dy = o1.reshape(b, DG, KK, H, W)
            dx = o2.reshape(b, DG, KK, H, W)
            mask = jax.nn.sigmoid(m).reshape(b, DG, KK, 1, H, W)
            ys = jnp.arange(H, dtype=x.dtype)[None, None, None, :, None]
            xs = jnp.arange(W, dtype=x.dtype)[None, None, None, None, :]
            py = ys + dy
            px = xs + dx
            xg = x.reshape(b, DG, CPG, H, W)
            sampled = jax.vmap(jax.vmap(_sample_group))(xg, py, px)
            y = sampled * mask
            y = y.reshape(b, C * KK, H, W)
            return jnp.einsum('bkhw,ok->bohw', y, w_conv)
        return _forward(x, w_off, b_off, w_conv)

    def _L1_conv_ref(x, g1, mem_kv, w_qkv, w_out, b_out, g2):
        import jax, jax.numpy as jnp
        import numpy as np
        EPS = 1e-12

        def _rms_norm(x, g):
            c = x.shape[1]
            n = jnp.maximum(jnp.linalg.norm(x, axis=1, keepdims=True), EPS)
            return x / n * g * c ** 0.5
        b, c, H, W = x.shape
        _, heads, dim_head, num_mem = mem_kv.shape
        n = H * W
        scale = dim_head ** (-0.5)
        xn = _rms_norm(x, g1)
        qkv = jnp.einsum('oc,bchw->bohw', w_qkv, xn)
        hidden = heads * dim_head
        q, k, v = jnp.split(qkv, 3, axis=1)
        q = q.reshape(b, heads, dim_head, n)
        k = k.reshape(b, heads, dim_head, n)
        v = v.reshape(b, heads, dim_head, n)
        mk = jnp.broadcast_to(mem_kv[0], (b, heads, dim_head, num_mem))
        mv = jnp.broadcast_to(mem_kv[1], (b, heads, dim_head, num_mem))
        k = jnp.concatenate([mk, k], axis=-1)
        v = jnp.concatenate([mv, v], axis=-1)
        q = jax.nn.softmax(q, axis=-2) * scale
        k = jax.nn.softmax(k, axis=-1)
        context = jnp.einsum('bhdn,bhen->bhde', k, v)
        out = jnp.einsum('bhde,bhdn->bhen', context, q)
        out = out.reshape(b, hidden, H, W)
        o = jnp.einsum('oc,bchw->bohw', w_out, out) + b_out[None, :, None, None]
        return _rms_norm(o, g2)

    def _gn(v, G=32, eps=1e-5):
        B_, C_, H_, W_ = v.shape
        g = v.reshape(B_, G, C_ // G, H_, W_)
        m = jnp.mean(g, axis=(2, 3, 4), keepdims=True)
        s = jnp.var(g, axis=(2, 3, 4), keepdims=True)
        return ((g - m) / jnp.sqrt(s + eps)).reshape(v.shape)

    def _ln_c(v, eps=1e-6):
        m = jnp.mean(v, axis=1, keepdims=True)
        s = jnp.var(v, axis=1, keepdims=True)
        return (v - m) / jnp.sqrt(s + eps)

    def _ln_t(v, eps=1e-5):
        m = jnp.mean(v, axis=-1, keepdims=True)
        s = jnp.var(v, axis=-1, keepdims=True)
        return (v - m) / jnp.sqrt(s + eps)

    def _to_tokens(v):
        B_, C_, H_, W_ = v.shape
        return v.reshape(B_, C_, H_ * W_).transpose(0, 2, 1)
    def _from_tokens(t, like):
        B_, C_, H_, W_ = like.shape
        return t.transpose(0, 2, 1).reshape(B_, C_, H_, W_)

    x = x + _L0_conv_ref(_gn(x), L0_conv_w_off, L0_conv_b_off, L0_conv_w_conv)
    x = x + _L1_conv_ref(_gn(x), L1_conv_g1, L1_conv_mem_kv, L1_conv_w_qkv, L1_conv_w_out, L1_conv_b_out, L1_conv_g2)
    return x


_drawn_inputs = setup_inputs


def setup_inputs(seed=0):
    import zlib

    import numpy as np

    out = dict(_drawn_inputs(seed))
    spreads = {'L0_conv_b_off': (0.0, 0.1),
     'L1_conv_g1': (1.0, 0.6),
     'L1_conv_b_out': (0.0, 0.1),
     'L1_conv_g2': (1.0, 0.2)}
    factors = {'L1_conv_mem_kv': 8.0}
    for name, (base, spread) in spreads.items():
        noise = np.random.default_rng([zlib.crc32(name.encode()), seed]).standard_normal(out[name].shape)
        drawn = base * np.exp(spread * noise) if base else spread * noise
        out[name] = jnp.asarray(drawn.astype(out[name].dtype))
    for name, factor in factors.items():
        out[name] = (out[name] * factor).astype(out[name].dtype)
    return out
```

```python
from contextlib import ExitStack

import concourse.bass as bass
import numpy as np
from concourse import mybir


NI, C, H, W = 8, 256, 64, 64
HW = H * W
P = 128
NH = C // P
KK = 9
R = 3
QR, QC = 8, 16
NT = W // QC
PR = QR - 2 * R
WIN = [(max(0, QC * t - R), min(W, QC * (t + 1) + R)) for t in range(NT)]
WOFF = [sum(b - a for a, b in WIN[:t]) for t in range(NT)]
WW = sum(b - a for a, b in WIN)
NE = 2 * R + 1
NG = 3
GK = KK // NG
GW = GK * PR * WW
NB = H // PR
MB = 2
NM = NB // MB
MP = MB * PR * W
NO = MB * NG
XR = H + 2 * R
PADR = H + 2
SX, SA = 16.0, 16.0
SW = 256.0
HEADS, DH = 4, 32
HID = HEADS * DH
MEM = 4
CH = 512
NC = HW // CH
RC = CH // W
EPS = 1e-5


def tables():
    p = np.arange(P)
    t = {}
    t["ident16"] = np.eye(P, dtype=np.float16)
    t["ident32"] = np.eye(P, dtype=np.float32)
    t["ones32"] = np.ones((P, P), np.float32)
    per = C // 32
    t["group_mean"] = ((p[:, None] // per == p[None] // per) / per).astype(np.float32)
    t["head_mask"] = (p[:, None] // DH == p[None] // DH).astype(np.float32)
    sel = np.zeros((P, 2, P), np.float32)
    for j in range(4):
        for k in range(KK):
            for e in range(NE):
                sel[32 * j + k, 0, k * NE + e] = 1
                sel[32 * j + 2 * KK + k, 1, k * NE + e] = 1
            sel[32 * j + KK + k, 0, 64 + k] = 1
            sel[32 * j + k, 0, 96 + k] = 1
    t["spread"] = sel
    sy = np.zeros((P, KK, PR, P), np.float16)
    for k in range(KK):
        for y in range(PR):
            for q in range(P):
                e = q // QC - y
                if 0 <= e < NE:
                    sy[k * NE + e, k, y, q] = 1
                    sy[64 + k * NE + e, k, y, q] = 1
    t["pick_y"] = sy
    sx = np.zeros((P, KK, P), np.float16)
    for k in range(KK):
        sx[64 + k, k] = 1
        sx[96 + k, k] = 1
        sx[0, k] = 1
    t["pick_x"] = sx
    t["window_column"] = np.tile(
        np.concatenate([SX * (np.arange(a, b) - QC * i) for i, (a, b) in enumerate(WIN)]), H
    ).astype(np.float16)[None]
    t["of_channel"] = (p[:, None] % 32 == np.arange(32)[None]).astype(np.float32)
    px = np.arange(PR * W)
    t["far_xy"] = np.stack([px[None] // W - p[:, None] // W, px[None] % W - p[:, None] % W], 1).astype(np.float32)
    t["far_rows"] = np.tile(float(PR) * (np.arange(2 * NB) - (NB - 1)), (P, 1)).astype(np.float32)
    small = np.zeros((P, 3), np.float32)
    small[:, 0] = -(p % QC)
    small[: KK * NE, 1] = -(p[: KK * NE] % NE - R)
    small[:, 2] = EPS
    t["small"] = small
    return t


TABLES = ["ident16", "ident32", "ones32", "group_mean", "head_mask", "spread", "pick_y", "pick_x",
          "window_column", "small", "of_channel", "far_xy", "far_rows"]


class Count:

    def __init__(self, eng, sem):
        self.eng, self.sem, self.base, self.n = eng, sem, 0, 0

    def at(self, base):
        self.base, self.n = base, 0

    def inc(self, ins):
        ins.then_inc(self.sem, 1)
        self.n += 1
        return self

    def wait(self):
        self.eng.wait_ge(self.sem, self.base + self.n)


def deform_attention(nc, ctx, ni, dram, out):
    f32, f16, i32 = mybir.dt.float32, mybir.dt.float16, mybir.dt.int32
    ALU = mybir.AluOpType
    ACT = mybir.ActivationFunctionType
    X = mybir.AxisListType.X
    ds = bass.ds

    def sb(name, shape, dt):
        return ctx.enter_context(nc.sbuf_tensor(name, shape, dt))

    def sem(name):
        return ctx.enter_context(nc.semaphore(name))

    x = sb("x", [P, NH, HW], f32)
    arena_x = sb("arena_x", [P, NH * PADR * W], f32)
    xp = arena_x[:, :].bitcast(f16).rearrange("p (s h n) -> p s h n", s=2, h=NH)
    q_soft = arena_x[:, 0:HW]
    vt = arena_x[:, HW:HW + NB * (HID + 1)].rearrange("p (t e) -> p t e", e=HID + 1)
    offs = sb("offs", [P, HW], f32)
    kt = offs[:, :].rearrange("p (t d) -> p t d", d=HID)
    vhat = sb("vhat", [P, H * WW], f16)
    dxw = sb("dxw", [P, H * WW], f16)
    wt = sb("wt", [P, KK * NH, 2, C], f16)
    wofft = sb("wofft", [P, KK * NH, 2, 32], f16)
    wqkvt = sb("wqkvt", [P, NH, 3 * HID], f32)
    woutt = sb("woutt", [P, C], f32)
    ident16 = sb("ident16", [P, P], f16)
    ident32 = sb("ident32", [P, P], f32)
    ones32 = sb("ones32", [P, P], f32)
    group_mean = sb("group_mean", [P, P], f32)
    head_mask = sb("head_mask", [P, P], f32)
    spread = sb("spread", [P, 2, P], f32)
    pick_y = sb("pick_y", [P, KK, PR, P], f16)
    pick_x = sb("pick_x", [P, KK, P], f16)
    small = sb("small", [P, 3], f32)
    of_channel = sb("of_channel", [P, 32], f32)
    far_xy = sb("far_xy", [P, 2, PR * W], f32)
    far_rows = sb("far_rows", [P, 2 * NB], f32)
    boff_all = sb("boff_all", [P, 3 * KK], f32)
    zero16 = sb("zero16", [P, P], f16)
    far_flag = sb("far_flag", [P, 1], i32)
    boff = sb("boff", [3 * KK, 1], f32)
    bias_r = sb("bias_r", [P, 2], f32)
    wmax = sb("wmax", [P, 2, 4], f32)
    wall = sb("wall", [P, 2, 4], f32)
    g1 = sb("g1", [P, NH], f32)
    g2 = sb("g2", [P, NH], f32)
    bout = sb("bout", [P, NH], f32)
    memk = sb("memk", [P, MEM], f32)
    memv = sb("memv", [MEM, HID + 1], f32)
    memv_raw = sb("memv_raw", [P, MEM], f32)
    st = [sb(f"stats{n}", [P, NH, NM, 6], f32) for n in range(2)]
    mv = sb("mv", [P, NH, 2], f32)
    gst = sb("gst", [P, 12, NH], f32)
    far_max = sb("far_max", [P, NC], f32)
    far_red = sb("far_red", [P, 4], f32)
    c1 = sb("c1", [P, 6, NB], f32)
    c2 = sb("c2", [P, 8, 16], f32)
    work = sb("work", [P, 10944], f32)

    def carve(at, n, dt):
        m = n if dt == f32 else n // 2
        v = work[:, at:at + m]
        return v if dt == f32 else v.bitcast(dt)

    xt = carve(0, 2 * NT * 512, f16).rearrange("p (u t c) -> p u t c", u=2, t=NT)
    S = carve(2048, 2 * NH * KK * MP, f16).rearrange("p (s h k n) -> p s h k n", s=2, h=NH, k=KK)
    t_abs = [carve(6656 + 496 * n, GW, f32) for n in range(1)]
    hat_x = [carve(7152 + 496 * n, GW, f32) for n in range(2)]
    a_full = [carve(8144 + 496 * n, GW, f32) for n in range(2)]
    a_hl = [[carve(9136 + 248 * (2 * n + s), GW, f16) for s in range(2)] for n in range(3)]
    far_py, far_px, far_m, far_hx, far_t, far_a = (carve(6656 + GK * P * n, GK * P, f32) for n in range(6))
    far_hl = [carve(6656 + 6 * GK * P + GK * P // 2 * n, GK * P, f16) for n in range(2)]
    xn_tmp = [carve(1024 * n, 1024, f32) for n in range(2)]
    stage = [carve(2048 + 512 * n, 1024, f16) for n in range(2)]
    r_abs, r_hat, r_sig, r_v, r_d = (carve(3072 + 2 * 328 * n, 656, f32) for n in range(5))
    an = [carve(1024 * n, 1024, f32).rearrange("p (h n) -> p h n", h=NH) for n in range(2)]
    sq = [carve(2048 + 1024 * n, 1024, f32).rearrange("p (h n) -> p h n", h=NH) for n in range(2)]
    qs = [carve(4096 + 512 * n, 512, f32) for n in range(2)]
    qe = [carve(5120 + 512 * n, 512, f32) for n in range(2)]
    ek = [carve(6144 + 512 * n, 512, f32) for n in range(2)]
    ekx = [carve(7168 + 512 * n, 512, f32) for n in range(2)]
    kmx = carve(8192, 512, f32)
    kmb = carve(8704, 128, f32)
    kred = carve(8832, 128, f32)
    kdiag = carve(8960, 128, f32)
    ctxn = carve(9088, 128, f32)
    ctxt = carve(9216, 128, f32)
    m2 = carve(9344, 256, f32)
    ekm = carve(9600, 8, f32)
    ekmt = carve(9616, 128, f32)
    odiag = [carve(9744 + 512 * n, 512, f32) for n in range(2)]
    wc_raw = x[:, :, :].rearrange("p h n -> p (h n)")[:, 0:NH * KK * C].rearrange("p (h n) -> p h n", h=NH)
    wc_hl = [arena_x[:, 4608 // 2 * s:4608 // 2 * (s + 1)].bitcast(f16).rearrange("p (h n) -> p h n", h=NH)
             for s in range(2)]
    wo_raw = x[:, :, :].rearrange("p h n -> p (h n)")[:, 4608:4608 + KK * C]
    wo_hl = [arena_x[:, 4608 + 1152 * s:4608 + 1152 * (s + 1)].bitcast(f16) for s in range(2)]
    wq_raw = work[:, 0:3 * C].rearrange("p (a c) -> p a c", a=3)
    wu_raw = work[:, 1024:1024 + NH * HID].rearrange("p (a c) -> p a c", a=NH)

    bank = [ctx.enter_context(nc.psum_tensor(f"bank{n}", [P, 512], f32)) for n in range(8)]
    xtd = nc.dram_tensor("xt_scratch", (XR, W, 2 * C), f16, kind="Internal").ap()

    S_ = {}

    def s(name):
        if name not in S_:
            S_[name] = sem(name)
        return S_[name]

    OPEN = 1
    OPENED = ["y_out", "xt_copied0", "xt_copied1", "xt_out0", "xt_out1", "xt_used0", "xt_used1", "far_used",
              "y_ready", "r_done", "sq_ready0", "sq_ready1", "qkv_ready0", "qkv_ready1", "ek_ready0", "ek_ready1",
              "conv0", "conv1", "conv2", "s_lo", "x1_ready", "hx_read", "far_a", "sq_used0", "sq_used1",
              "q_t0", "q_t1", "ctx_done0", "ctx_done1", "qkv_copied", "q_t_copied", "o_copied", "o_sqrt", "o_scaled"]

    block = ctx.enter_context(nc.Block())
    BANK_HX, BANK_HY, BANK_S, BANK_O = 0, (1, 2), (3, 5), 7
    NWT = KK * NH * 4 // 8
    N_CONST = 23
    NWO = 5

    def stand(eng):
        eng.sem_inc(s(f"stood_{eng.engine.name}"), 1)

    def path_counts(eng):
        regs = [eng.alloc_register(name) for name in ("far_images", "near_images")]
        for reg in regs:
            eng.reg_mov(reg, 0)
        return regs

    def which_path(eng, i, counts):
        eng.wait_ge(s("far_flag_ready"), i + 1)
        stand(eng)
        flag = eng.value_load(far_flag[0:1, 0:1], min_val=0, max_val=1)
        return flag > 0, *(eng.snap(reg, min_val=0, max_val=ni) for reg in counts)

    @block.sync
    def _(sp):
        for name, tile in (("ident16", ident16), ("ident32", ident32), ("ones32", ones32),
                           ("group_mean", group_mean), ("head_mask", head_mask), ("spread", spread),
                           ("pick_y", pick_y), ("pick_x", pick_x), ("small", small), ("of_channel", of_channel),
                           ("far_xy", far_xy), ("far_rows", far_rows)):
            full = tile[tuple(slice(None) for _ in tile.shape)]
            sp.dma_start(full, dram[name]).then_inc(s("const_in"), 16)
        sp.dma_start(boff_all[:, :], dram["L0_conv_b_off"].rearrange("(o n) -> o n", o=1).to_broadcast([P, 3 * KK])
                     ).then_inc(s("const_in"), 16)
        sp.dma_start(wc_raw, dram["L0_conv_w_conv"].rearrange("(h p) n -> p h n", p=P)).then_inc(s("wc_in"), 16)
        sp.wait_ge(s("zeroed"), 1)
        sp.dma_start(wo_raw[0:3 * KK, :], dram["L0_conv_w_off"].rearrange("o c a b -> o (c a b)")).then_inc(s("wo_in"), 16)
        sp.dma_start(wq_raw, dram["L1_conv_w_qkv"].rearrange("(a p) c -> p a c", p=P)).then_inc(s("wa_in"), 16)
        sp.dma_start(wu_raw, dram["L1_conv_w_out"].rearrange("(a p) c -> p a c", p=P)).then_inc(s("wa_in"), 16)
        sp.dma_start(boff[:, :], dram["L0_conv_b_off"].rearrange("(p n) -> p n", n=1)).then_inc(s("const_in"), 16)
        for tile, name in ((g1, "L1_conv_g1"), (g2, "L1_conv_g2")):
            for h in range(NH):
                sp.dma_start(tile[:, h:h + 1], dram[name][0, h * P:(h + 1) * P, 0, :]).then_inc(s("const_in"), 16)
        for h in range(NH):
            sp.dma_start(bout[:, h:h + 1], dram["L1_conv_b_out"][h * P:(h + 1) * P].rearrange("(p n) -> p n", n=1)
                         ).then_inc(s("const_in"), 16)
        mkv = dram["L1_conv_mem_kv"].rearrange("a h d m -> a (h d) m")
        sp.dma_start(memk[:, :], mkv[0]).then_inc(s("const_in"), 16)
        sp.dma_start(memv_raw[:, :], mkv[1]).then_inc(s("const_in"), 16)
        for r0 in (0, XR - R):
            sp.dma_start(xtd[r0:r0 + R, :, :].rearrange("r (a w) c -> (r a) (w c)", a=32),
                         vhat[0:R * 32, 0:2 * W * C // 32]).then_inc(s("zero_rows"), 16)
        sp.dma_start(dxw[0:1, :], dram["window_column"]).then_inc(s("const_in"), 16)

        counts = path_counts(sp)
        with sp.Fori(0, ni) as i:
            sp.wait_ge(s("prepared"), 1)
            sp.wait_ge(s("y_out"), i * (16 * NC) + OPEN)
            stand(sp)
            for h in range(NH):
                sp.dma_start(x[:, h, :], dram["x_v"][i, h]).then_inc(s(f"x_in{h}"), 16)
            with sp.Fori(0, NB // 4) as t:
                for u in range(2):
                    sp.wait_ge(s(f"xt_copied{u}"), i * (NB // 4) + t + 1 + OPEN)
                    dst = xtd[ds(R + 8 * t + 4 * u, 4), :, :]
                    sp.dma_start(dst.rearrange("(m a) w c -> (a w) m c", a=2),
                                 stage[u].rearrange("p (m c) -> p m c", m=2)).then_inc(s(f"xt_out{u}"), 16)
            for u in range(2):
                sp.wait_ge(s(f"xt_out{u}"), (i + 1) * (16 * NB // 4) + OPEN)
            sp.wait_ge(s("r_done"), (i + 1) * NC + OPEN)
            is_far, far, near = which_path(sp, i, counts)
            with sp.If(is_far):
                with sp.Fori(0, NM * NO) as g:
                    with sp.Fori(0, NB) as q:
                        sp.wait_ge(s("far_used"), (far * (NM * NO) + g) * NB + q + OPEN)
                        sp.dma_start(xt[:, 0, 0, :], xtd[ds(R + PR * q, PR), :, :]).then_inc(s("far_in"), 16)
                sp.reg_add(counts[0], counts[0], 1)
            with sp.Else():
                with sp.Fori(0, NM) as j:
                    for u in range(2):
                        sp.wait_ge(s(f"xt_used{u}"), i * NM + j + OPEN)
                        for t in range(NT):
                            src = xtd[ds(2 * PR * j + PR * u, QR), QC * t:QC * (t + 1), :]
                            sp.dma_start(xt[:, u, t, :], src).then_inc(s(f"xt_in{u}"), 16)
            with sp.Fori(0, NC) as c:
                sp.wait_ge(s("y_ready"), i * NC + c + 1 + OPEN)
                sp.dma_start(out[i].rearrange("h p n -> p h n")[:, :, ds(c * CH, CH)],
                             x[:, :, ds(c * CH, CH)]).then_inc(s("y_out"), 16)
        sp.wait_ge(s("y_out"), ni * 16 * NC + OPEN)

    @block.gpsimd
    def _(pool):
        amax = bass.bass_isa.ReduceOp.max
        for name in OPENED:
            pool.sem_inc(s(name), OPEN)
        nc.gpsimd.memset(wo_raw, 0.0)
        nc.gpsimd.memset(dxw[:, :], 0.0)
        nc.gpsimd.memset(far_max[:, :], 0.0)
        nc.gpsimd.memset(memv[:, :], 1.0)
        nc.gpsimd.memset(zero16[:, :], 0.0)
        nc.gpsimd.memset(vhat[:, :], 0.0).then_inc(s("zeroed"), 1)
        for n in range(2):
            pool.wait_ge(s("wmax_ready"), n + 1)
            nc.gpsimd.partition_all_reduce(wall[:, n, 0:1], wmax[:, n, 0:1], P, amax).then_inc(s("wall_ready"), 1)
        with pool.Fori(0, ni) as i:
            pool.wait_ge(s("prepared"), 1)
            pool.wait_ge(s("y_ready"), i * NC + OPEN)
            stand(pool)
            for part in range(2):
                for h in range(NH):
                    v = xp[:, part, h]
                    nc.gpsimd.memset(v[:, 0:W], 0.0)
                    nc.gpsimd.memset(v[:, (PADR - 1) * W:PADR * W], 0.0).then_inc(s("border"), 1)
            pool.wait_ge(s("far_max_ready"), i + 1)
            stand(pool)
            nc.gpsimd.partition_all_reduce(far_red[:, 1:2], far_red[:, 0:1], P, amax).then_inc(s("far_all"), 1)
            pool.wait_ge(s("off_ready"), (i + 1) * NC)
            stand(pool)
            nc.gpsimd.memset(vt[:, :, HID:HID + 1], 1.0).then_inc(s("v_ones"), 1)

    def gn_dve(layer, d, i):
        n_st = NC if layer == 0 else NM
        stand(nc.vector)
        for h in range(NH):
            d.inc(nc.vector.bn_aggr(mv[:, h, :], st[layer][:, h, 0:n_st, :]))
        d.wait()
        d.inc(nc.vector.tensor_copy(gst[:, 0, :], mv[:, :, 0]))
        d.inc(nc.vector.tensor_tensor(gst[:, 1, :], mv[:, :, 0], mv[:, :, 0], ALU.mult))
        d.wait()
        nc.vector.tensor_tensor(gst[:, 1, :], gst[:, 1, :], mv[:, :, 1], ALU.add).then_inc(s(f"gn_sums{layer}"), 1)
        nc.vector.wait_ge(s(f"gn_means{layer}"), i + 1)
        d.inc(nc.vector.tensor_copy(gst[:, 2:4, :], bank[0][:, 0:4].rearrange("p (a h) -> p a h", h=NH)))
        d.wait()
        d.inc(nc.vector.tensor_tensor(gst[:, 4, :], gst[:, 2, :], gst[:, 2, :], ALU.mult))
        d.wait()
        d.inc(nc.vector.tensor_tensor(gst[:, 4, :], gst[:, 3, :], gst[:, 4, :], ALU.subtract))
        d.wait()
        nc.vector.tensor_scalar(gst[:, 4, :], gst[:, 4, :], 0.0, EPS, ALU.max, ALU.add).then_inc(s(f"gn_var{layer}"), 1)
        nc.vector.wait_ge(s(f"gn_sqrt{layer}"), i + 1)
        d.inc(nc.vector.reciprocal(gst[:, 6, :], gst[:, 5, :]))
        d.wait()
        d.inc(nc.vector.tensor_tensor(gst[:, 7, :], gst[:, 6, :], gst[:, 6, :], ALU.mult))
        d.wait()
        d.inc(nc.vector.tensor_tensor(gst[:, 7, :], gst[:, 7, :], gst[:, 4, :], ALU.mult))
        d.wait()
        d.inc(nc.vector.tensor_scalar(gst[:, 7, :], gst[:, 7, :], -0.5, 1.5, ALU.mult, ALU.add))
        d.wait()
        sc = SX if layer == 0 else 1.0
        d.inc(nc.vector.scalar_tensor_tensor(gst[:, 9, :], gst[:, 6, :], sc, gst[:, 7, :], ALU.mult, ALU.mult))
        d.wait()
        d.inc(nc.vector.scalar_tensor_tensor(gst[:, 10, :], gst[:, 2, :], -1.0, gst[:, 9, :], ALU.mult, ALU.mult))
        d.wait()

    GN_STEPS = 2 + 2 + 1 + 2 + 4 + 2

    @block.vector
    def _(dve):
        d = Count(dve, s("dve_prep"))
        def scale_of(n, rows, raw, back):
            d.inc(nc.vector.memset(wmax[:, n, :], 0.0))
            d.wait()
            nc.vector.tensor_reduce(wmax[rows, n, 0:1], raw, mybir.AxisListType.XY if len(raw.shape) == 3 else X,
                                    ALU.max, apply_absolute_value=True).then_inc(s("wmax_ready"), 1)
            dve.wait_ge(s("wall_ready"), n + 1)
            d.inc(nc.vector.tensor_scalar(wall[:, n, 1:2], wall[:, n, 0:1], 1e-30, None, ALU.max))
            d.wait()
            d.inc(nc.vector.reciprocal(wall[:, n, 2:3], wall[:, n, 1:2]))
            d.inc(nc.vector.tensor_scalar(wall[:, n, 3:4], wall[:, n, 1:2], back, None, ALU.mult))
            d.wait()
            d.inc(nc.vector.tensor_scalar(wall[:, n, 2:3], wall[:, n, 2:3], SW, None, ALU.mult))
            d.wait()

        dve.wait_ge(s("wc_in"), 16)
        scale_of(0, slice(0, P), wc_raw, 1.0 / (SW * SX * SA))
        d.inc(nc.vector.tensor_scalar(wc_raw, wc_raw, wall[:, 0, 2:3], None, ALU.mult))
        d.wait()
        d.inc(nc.vector.tensor_copy(wc_hl[0], wc_raw))
        d.wait()
        nc.vector.tensor_tensor(wc_hl[1], wc_raw, wc_hl[0], ALU.subtract).then_inc(s("wc_split"), 1)
        dve.wait_ge(s("wo_in"), 16)
        scale_of(1, slice(0, P), wo_raw, 1.0 / (SW * SX))
        wo_v = wo_raw.rearrange("p (c t) -> p t c", t=KK)
        wo_hi = wo_hl[0].rearrange("p (t c) -> p t c", t=KK)
        wo_lo = wo_hl[1].rearrange("p (t c) -> p t c", t=KK)
        d.inc(nc.vector.tensor_scalar(wo_raw, wo_raw, wall[:, 1, 2:3], None, ALU.mult))
        d.wait()
        d.inc(nc.vector.tensor_copy(wo_hi, wo_v))
        d.wait()
        nc.vector.tensor_tensor(wo_lo, wo_v, wo_hi, ALU.subtract).then_inc(s("wo_split"), 1)
        dve.wait_ge(s("const_in"), 16 * N_CONST)
        for e in range(NWT):
            dve.wait_ge(s("wt_ready"), e + 1)
            nc.vector.tensor_copy(wt[:, 2 * e:2 * e + 2, :, :].rearrange("p k a c -> p (k a c)"),
                                  bank[e % 2][:, :].bitcast(f16)).then_inc(s("wt_copied"), 1)
        for e in range(NWO):
            dve.wait_ge(s("wt_ready"), NWT + e + 1)
            m = min(8, 2 * KK * NH - 8 * e)
            nc.vector.tensor_copy(wofft[:, 4 * e:4 * e + m // 2, :, :].rearrange("p k a c -> p (k a c)"),
                                  bank[(NWT + e) % 2][:, :].bitcast(f16)[:, 0:32 * m]).then_inc(s("wt_copied"), 1)
        for a in range(3):
            for h in range(NH):
                n = a * NH + h
                dve.wait_ge(s("wa_ready"), n + 1)
                nc.vector.tensor_scalar(wqkvt[:, h, a * P:(a + 1) * P], bank[2 + n % 2][:, 0:P], g1[:, h:h + 1],
                                        float(C) ** 0.5, ALU.mult, ALU.mult).then_inc(s("wa_copied"), 1)
        for h in range(NH):
            n = 6 + h
            dve.wait_ge(s("wa_ready"), n + 1)
            nc.vector.tensor_copy(woutt[:, h * P:(h + 1) * P], bank[2 + n % 2][:, 0:P]).then_inc(s("wa_copied"), 1)
        dve.wait_ge(s("wa_ready"), 9)
        dve.wait_ge(s("zeroed"), 1)
        d.inc(nc.vector.tensor_copy(memv[:, 0:HID], bank[2][0:MEM, 0:P]))
        dve.wait_ge(s("bias_rows"), 1)
        d.inc(nc.vector.tensor_copy(bias_r[:, :], bank[3][:, 0:2]))
        d.wait()
        nc.vector.tensor_tensor(bias_r[:, 0:1], bias_r[:, 0:1], small[:, 1:2], ALU.add).then_inc(s("prepared"), 1)

        gd = [Count(dve, s(f"dve_gn{n}")) for n in range(2)]
        rd, bd, xd = Count(dve, s("dve_r")), Count(dve, s("dve_b")), Count(dve, s("dve_x"))
        qd, kd, od = Count(dve, s("dve_q")), Count(dve, s("dve_k")), Count(dve, s("dve_o"))
        counts = path_counts(dve)
        with dve.Fori(0, ni) as i:
            for h in range(NH):
                dve.wait_ge(s(f"x_in{h}"), (i + 1) * 16)
                for c in range(NC):
                    nc.vector.bn_stats(st[0][:, h, c, :], x[:, h, c * CH:(c + 1) * CH]).then_inc(s("st_ready"), 1)
            dve.wait_ge(s("st_ready"), (i + 1) * (NH * NC))
            gd[0].at(i * GN_STEPS)
            gn_dve(0, gd[0], i)
            dve.wait_ge(s("border"), (i + 1) * 4)
            stand(dve)
            with dve.Fori(0, 4) as r:
                for h in range(NH):
                    nc.vector.tensor_scalar(xn_tmp[h], x[:, h, ds(r * 1024, 1024)], gst[:, 9, h:h + 1],
                                            gst[:, 10, h:h + 1], ALU.mult, ALU.add).then_inc(s("xn_ready"), 1)
                for h in range(NH):
                    dve.wait_ge(s("xn_hi"), i * 8 + r * 2 + h + 1)
                    dst = [xp[:, part, h, ds(r * 1024 + W, 1024)] for part in range(2)]
                    nc.vector.tensor_tensor(dst[1], xn_tmp[h], dst[0],
                                            ALU.subtract).then_inc(s("xn_lo"), 1)
                dve.wait_ge(s("xn_lo"), i * 8 + r * 2 + 2)
            with dve.Fori(0, NB // 4) as t:
                dve.wait_ge(s("xt_ready1"), i * (NB // 4) + t + 1)
                dve.wait_ge(s("xt_out1"), (i * (NB // 4) + t) * 16 + OPEN)
                nc.vector.tensor_copy(stage[1], bank[1][:, :].bitcast(f16)).then_inc(s("xt_copied1"), 1)
            R_STEPS = 8
            with dve.Fori(0, NC) as c:
                rd.at((i * NC + c) * R_STEPS)
                cols = ds(c * (RC * WW), RC * WW)
                dve.wait_ge(s("r_ready"), i * NC + c + 1)
                r1 = [bank[4 + n][64:105, 0:4 * WW] for n in range(2)]
                rdv = r_d[64:105, :].rearrange("p (b n) -> p b n", b=2)
                for n in range(2):
                    rd.inc(nc.vector.tensor_scalar(rdv[:, n, :], r1[n], bias_r[64:105, 0:1], 8.0, ALU.add, ALU.min))
                rd.wait()
                rd.inc(nc.vector.tensor_scalar(r_d[64:105, :], r_d[64:105, :], -8.0, SX, ALU.max, ALU.mult))
                rd.wait()
                rd.inc(nc.vector.tensor_reduce(far_max[64:105, ds(c, 1)], r_d[64:105, :], X, ALU.max,
                                               apply_absolute_value=True))
                rd.inc(nc.vector.tensor_copy(dxw[64:64 + KK, cols], r_d[64:64 + KK, :]))
                rd.wait()
                rd.inc(nc.vector.tensor_tensor(dxw[96:96 + KK, cols], r_d[64:64 + KK, :], dxw[64:64 + KK, cols],
                                               ALU.subtract))
                dve.wait_ge(s("r_act"), i * NC + c + 1)
                rd.inc(nc.vector.tensor_tensor(r_v[0:63, :], r_hat[0:63, :], r_sig[0:63, :], ALU.mult))
                rd.wait()
                rd.inc(nc.vector.tensor_copy(vhat[0:63, cols], r_v[0:63, :]))
                rd.wait()
                nc.vector.tensor_tensor(vhat[64:127, cols], r_v[0:63, :], vhat[0:63, cols],
                                        ALU.subtract).then_inc(s("r_done"), 1)
            dve.wait_ge(s("r_done"), (i + 1) * NC + OPEN)
            nc.vector.tensor_reduce(far_red[:, 0:1], far_max[:, :], X, ALU.max).then_inc(s("far_max_ready"), 1)
            dve.wait_ge(s("far_all"), i + 1)
            nc.vector.tensor_scalar(far_flag[:, :], far_red[:, 1:2], R * SX, None, ALU.is_gt).then_inc(s("far_flag_ready"), 1)

            def front(f, o):
                dve.wait_ge(s("hatx_ready"), f + 1)
                dve.wait_ge(s("hy_ready"), f + 1)
                nc.vector.tensor_tensor(a_full[o % 2], hat_x[o % 2], bank[BANK_HY[o % 2]][:, 0:GW],
                                        ALU.mult).then_inc(s("a_full"), 1)
                dve.wait_ge(s("a_hi"), f + 1)
                nc.vector.tensor_tensor(a_hl[o % 3][1], a_full[o % 2], a_hl[o % 3][0],
                                        ALU.subtract).then_inc(s("a_lo"), 1)

            def sampled_psum(o):
                b = BANK_S[o % 2]
                return [bank[b + h][:, 0:GK * P].rearrange("p (k n) -> p k n", k=GK) for h in range(NH)]

            def back(f, o):
                u, g = o % MB, o // MB
                dve.wait_ge(s("s_hi"), f + 1)
                src = sampled_psum(o)
                for h in range(NH):
                    k0, n0 = g * GK, u * P
                    ins = nc.vector.tensor_tensor(S[:, 1, h, k0:k0 + GK, n0:n0 + P], src[h],
                                                  S[:, 0, h, k0:k0 + GK, n0:n0 + P], ALU.subtract)
                ins.then_inc(s("s_lo"), 1)

            def macro(m, last):
                for o in range(NO):
                    if o + 2 < NO or not last:
                        front((near * NM + m) * NO + o + 2, o + 2)
                    back((i * NM + m) * NO + o, o)
                add_conv(m)

            def far_group(m, n, o):
                g = o // MB
                dve.wait_ge(s("far_spread"), n + 1)
                for k in range(GK):
                    cols = slice(k * P, (k + 1) * P)
                    for b, dst, ch in ((0, far_py, g * GK + k), (1, far_px, KK + g * GK + k)):
                        ins = nc.vector.scalar_tensor_tensor(dst[:, cols], bank[b][:, cols], boff_all[:, ch:ch + 1],
                                                             far_xy[:, b, :], ALU.add, ALU.add)
                ins.then_inc(s("far_coords"), 1)
                dve.wait_ge(s("far_hat"), n + 1)
                nc.vector.tensor_tensor(far_hx, far_hx, far_m, ALU.mult).then_inc(s("far_hx_ready"), 1)
                dve.wait_ge(s("far_hx_ready"), n + 1)
                stand(dve)
                with dve.Fori(0, NB) as q:
                    t = n * NB + q
                    dve.wait_ge(s("far_hy"), t + 1)
                    dve.wait_ge(s("far_used"), t + OPEN)
                    nc.vector.tensor_tensor(far_a, far_t, far_hx, ALU.mult).then_inc(s("far_a"), 1)
                    dve.wait_ge(s("far_a"), t + 1 + OPEN)
                    nc.vector.tensor_copy(far_hl[0], far_a).then_inc(s("far_a_hi"), 1)
                    dve.wait_ge(s("far_a_hi"), t + 1)
                    nc.vector.tensor_tensor(far_hl[1], far_a, far_hl[0], ALU.subtract).then_inc(s("far_a_lo"), 1)

            def far_macro(m):
                for o in range(NO):
                    far_group(m, (far * NM + m) * NO + o, o)
                    back((i * NM + m) * NO + o, o)
                add_conv(m)

            def add_conv(m):
                dve.wait_ge(s("conv2"), i * NM + m + 1 + OPEN)
                for h in range(NH):
                    xs = x[:, h, ds(m * MP, MP)]
                    ins = nc.vector.scalar_tensor_tensor(xs, bank[BANK_O][:, h * MP:(h + 1) * MP], wall[:, 0, 3:4], xs,
                                                         ALU.mult, ALU.add)
                ins.then_inc(s("x1_ready"), 1)
                dve.wait_ge(s("x1_ready"), i * NM + m + 1 + OPEN)
                for h in range(NH):
                    ins = nc.vector.bn_stats(st[1][:, h, ds(m, 1), :], x[:, h, ds(m * MP, MP)])
                ins.then_inc(s("st1_ready"), 1)

            is_far, far, near = which_path(dve, i, counts)
            with dve.If(is_far):
                with dve.Fori(0, NM) as m:
                    far_macro(m)
                dve.reg_add(counts[0], counts[0], 1)
            with dve.Else():
                for o in range(2):
                    front(near * (NM * NO) + o, o)
                with dve.Fori(0, NM - 1) as m:
                    macro(m, False)
                macro(NM - 1, True)
                dve.reg_add(counts[1], counts[1], 1)

            dve.wait_ge(s("st1_ready"), (i + 1) * NM)
            gd[1].at(i * GN_STEPS)
            gn_dve(1, gd[1], i)

            def normalized(slot, c):
                for h in range(NH):
                    ins = nc.vector.tensor_scalar(an[slot][:, h, :], x[:, h, ds(c * CH, CH)], gst[:, 9, h:h + 1],
                                                  gst[:, 10, h:h + 1], ALU.mult, ALU.add)
                ins.then_inc(s("an_ready"), 1)

            stand(dve)
            with dve.Fori(0, NC // 2) as c:
                for u in range(2):
                    dve.wait_ge(s(f"sq_ready{u}"), i * (NC // 2) + c + OPEN)
                    normalized(u, 2 * c + u)
            xd.at(i * 2)
            dve.wait_ge(s("norm_sqrt"), i + 1)
            xd.inc(nc.vector.memset(kmx, -3.0e38))
            xd.inc(nc.vector.tensor_scalar(c1[:, 1, :], c1[:, 0, :], 1e-12, None, ALU.max))
            xd.wait()
            nc.vector.reciprocal(c1[:, 2, :], c1[:, 1, :]).then_inc(s("rnorm"), 1)
            dve.wait_ge(s("rnorm"), i + 1)
            Q_STEPS = 4
            stand(dve)
            with dve.Fori(0, NC // 2) as c:
                for u in range(2):
                    n = i * NC + 2 * c + u
                    dve.wait_ge(s(f"qkv_ready{u}"), i * (NC // 2) + c + OPEN)
                    normalized(u, 2 * c + u)
                    qd.at(n * Q_STEPS)
                    dve.wait_ge(s("qkv_copied"), n + 1 + OPEN)
                    q3 = qs[u].rearrange("p (g d) -> p g d", d=DH)
                    e3 = qe[u].rearrange("p (g d) -> p g d", d=DH)
                    mx, sm, rs = c2[:, 3 * u, :], c2[:, 3 * u + 1, :], c2[:, 3 * u + 2, :]
                    def wide(v):
                        return v.rearrange("p (g o) -> p g o", o=1).to_broadcast([P, 16, DH])
                    qd.inc(nc.vector.tensor_reduce(mx, q3, X, ALU.max))
                    qd.inc(nc.vector.tensor_tensor(kmx, kmx, kt[:, ds((2 * c + u) * 4, 4), :].rearrange("p t d -> p (t d)"),
                                                   ALU.max))
                    qd.wait()
                    nc.vector.tensor_tensor(q3, q3, wide(mx), ALU.subtract).then_inc(s("q_shifted"), 1)
                    dve.wait_ge(s("q_exp"), n + 1)
                    qd.inc(nc.vector.tensor_reduce(sm, e3, X, ALU.add))
                    qd.wait()
                    qd.inc(nc.vector.reciprocal(rs, sm))
                    qd.wait()
                    nc.vector.tensor_tensor(e3, e3, wide(rs), ALU.mult).then_inc(s("q_ready"), 1)
            kd.at(i * 4)
            nc.vector.tensor_reduce(kred, kmx.rearrange("p (t d) -> p d t", t=4), X, ALU.max).then_inc(s("kred_ready"), 1)
            dve.wait_ge(s("kred_t"), i + 1)
            kd.inc(nc.vector.tensor_reduce(c2[:, 6, 0:1], bank[6][:, 0:P], X, ALU.max))
            kd.inc(nc.vector.tensor_reduce(c2[:, 6, 1:2], memk[:, :], X, ALU.max))
            kd.wait()
            kd.inc(nc.vector.tensor_tensor(c2[:, 6, 2:3], c2[:, 6, 0:1], c2[:, 6, 1:2], ALU.max))
            kd.wait()
            kd.inc(nc.vector.tensor_scalar(c2[:, 6, 3:4], c2[:, 6, 2:3], -1.0, None, ALU.mult))
            kd.wait()
            nc.vector.tensor_scalar(kdiag, ident32[:, :], c2[:, 6, 2:3], None, ALU.mult).then_inc(s("kdiag_ready"), 1)
            dve.wait_ge(s("kmb_ready"), i + 1)
            nc.vector.tensor_copy(kmb, bank[6][:, 0:P]).then_inc(s("kmb_copied"), 1)
            dve.wait_ge(s("kmb_copied"), i + 1)
            stand(dve)
            with dve.Fori(0, NC // 2) as c:
                for u in range(2):
                    dve.wait_ge(s(f"ek_ready{u}"), i * (NC // 2) + c + OPEN)
                    nc.vector.tensor_tensor(ekx[u].rearrange("p (t d) -> p t d", t=4), kt[:, ds((2 * c + u) * 4, 4), :],
                                            kmb.rearrange("p (o d) -> p o d", o=1).to_broadcast([P, 4, HID]),
                                            ALU.subtract).then_inc(s("k_shifted"), 1)
            dve.wait_ge(s("ekm_t"), i + 1)
            nc.vector.tensor_copy(ekmt[0:MEM, :], bank[6][0:MEM, 0:P]).then_inc(s("ekmt_ready"), 1)
            dve.wait_ge(s("ctx_ready"), i + 1)
            od.at(i * 2)
            od.inc(nc.vector.reciprocal(c2[:, 6, 4:5], bank[7][:, HID:HID + 1]))
            od.wait()
            od.inc(nc.vector.tensor_scalar(ctxn, bank[7][:, 0:HID], c2[:, 6, 4:5], float(DH) ** -0.5, ALU.mult, ALU.mult))
            od.wait()
            nc.vector.tensor_tensor(ctxn, ctxn, head_mask[:, :], ALU.mult).then_inc(s("ctxn_ready"), 1)
            dve.wait_ge(s("ctx_t"), i + 1)
            nc.vector.tensor_copy(ctxt, bank[6][:, 0:P]).then_inc(s("ctxt_ready"), 1)
            dve.wait_ge(s("m2_psum"), i + 1)
            nc.vector.tensor_copy(m2, bank[6][:, 0:C]).then_inc(s("m2_ready"), 1)
            O_STEPS = 2
            stand(dve)
            with dve.Fori(0, NC // 2) as c:
                for u in range(2):
                    n = i * NC + 2 * c + u
                    oc = Count(dve, s("dve_oc"))
                    oc.at(n * O_STEPS)
                    dve.wait_ge(s("o_sqrt"), n + 1 + OPEN)
                    oc.inc(nc.vector.tensor_scalar(c1[:, 4, 4 * u:4 * u + 4], c1[:, 3, 4 * u:4 * u + 4],
                                                   1e-12 / float(C) ** 0.5, None, ALU.max))
                    oc.wait()
                    oc.inc(nc.vector.reciprocal(c1[:, 5, 4 * u:4 * u + 4], c1[:, 4, 4 * u:4 * u + 4]))
                    oc.wait()
                    for t in range(4):
                        ins = nc.vector.tensor_scalar(odiag[u][:, t * P:(t + 1) * P], ident32[:, :],
                                                      c1[:, 5, 4 * u + t:4 * u + t + 1], None, ALU.mult)
                    ins.then_inc(s("odiag_ready"), 1)
                    dve.wait_ge(s("rb_ready"), n + 1)
                    for h in range(NH):
                        ins = nc.vector.tensor_tensor(an[u][:, h, :], an[u][:, h, :], bank[4][:, :], ALU.mult)
                    ins.then_inc(s("o_scaled"), 1)
                    dve.wait_ge(s("o_scaled"), n + 1 + OPEN)
                    for h in range(NH):
                        xs = x[:, h, ds((2 * c + u) * CH, CH)]
                        ins = nc.vector.scalar_tensor_tensor(xs, an[u][:, h, :], g2[:, h:h + 1], xs, ALU.mult, ALU.add)
                    ins.then_inc(s("y_ready"), 1)

    @block.scalar
    def _(act):
        act.wait_ge(s("prepared"), 1)
        act.wait_ge(s("const_in"), 16 * N_CONST)
        ra = Count(act, s("act_r"))
        counts = path_counts(act)
        with act.Fori(0, ni) as i:
            act.wait_ge(s("gn_var0"), i + 1)
            nc.scalar.activation(gst[:, 5, :], gst[:, 4, :], ACT.Sqrt).then_inc(s("gn_sqrt0"), 1)
            act.wait_ge(s("border"), (i + 1) * 4)
            stand(act)
            with act.Fori(0, 4) as r:
                for h in range(NH):
                    act.wait_ge(s("xn_ready"), i * 8 + r * 2 + h + 1)
                    nc.scalar.activation(xp[:, 0, h, ds(r * 1024 + W, 1024)], xn_tmp[h],
                                         ACT.Copy).then_inc(s("xn_hi"), 1)
            with act.Fori(0, NB // 4) as t:
                act.wait_ge(s("xt_ready0"), i * (NB // 4) + t + 1)
                act.wait_ge(s("xt_out0"), (i * (NB // 4) + t) * 16 + OPEN)
                nc.scalar.activation(stage[0], bank[0][:, :].bitcast(f16), ACT.Copy).then_inc(s("xt_copied0"), 1)
            for c in range(NC):
                act.wait_ge(s("off_ready"), i * NC + c + 1)
                nc.scalar.activation(offs[:, c * CH:(c + 1) * CH], bank[2 + c % 2][:, :], ACT.Copy,
                                     scale=wall[:, 1, 3:4]).then_inc(s("off_copied"), 1)
            with act.Fori(0, NC) as c:
                ra.at((i * NC + c) * 4)
                act.wait_ge(s("r_ready"), i * NC + c + 1)
                act.wait_ge(s("r_done"), i * NC + c + OPEN)
                av = r_abs[0:63, :].rearrange("p (b n) -> p b n", b=2)
                sv = r_sig[0:63, :].rearrange("p (b n) -> p b n", b=2)
                for n in range(2):
                    ra.inc(nc.scalar.activation(av[:, n, :], bank[4 + n][0:63, 0:4 * WW], ACT.Abs, bias=bias_r[0:63, 0:1]))
                ra.wait()
                ra.inc(nc.scalar.activation(r_hat[0:63, :], r_abs[0:63, :], ACT.Relu, bias=SA, scale=-SA))
                ra.inc(nc.scalar.activation(sv[:, 0, :], bank[6][0:63, 0:4 * WW], ACT.Sigmoid, bias=bias_r[0:63, 1:2]))
                ra.wait()
                nc.scalar.activation(sv[:, 1, :], bank[7][0:63, 0:4 * WW], ACT.Sigmoid,
                                     bias=bias_r[0:63, 1:2]).then_inc(s("r_act"), 1)

            def front(f, o):
                act.wait_ge(s("hx_ready"), f + 1)
                nc.scalar.activation(t_abs[0], bank[BANK_HX][:, 0:GW], ACT.Abs, bias=small[:, 0:1],
                                     scale=1.0 / SX).then_inc(s("hx_read"), 1)
                act.wait_ge(s("hx_read"), f + 1 + OPEN)
                nc.scalar.activation(hat_x[o % 2], t_abs[0], ACT.Relu, bias=1.0, scale=-1.0).then_inc(s("hatx_ready"), 1)
                act.wait_ge(s("a_full"), f + 1)
                nc.scalar.activation(a_hl[o % 3][0], a_full[o % 2], ACT.Copy).then_inc(s("a_hi"), 1)

            def back(f, o):
                u, g = o % MB, o // MB
                act.wait_ge(s("sampled"), f + 1)
                for h in range(NH):
                    src = bank[BANK_S[o % 2] + h][:, 0:GK * P].rearrange("p (k n) -> p k n", k=GK)
                    ins = nc.scalar.activation(S[:, 0, h, g * GK:(g + 1) * GK, u * P:(u + 1) * P], src, ACT.Copy)
                ins.then_inc(s("s_hi"), 1)

            def far_group(m, n, o):
                g = o // MB
                act.wait_ge(s("far_spread"), n + 1)
                for k in range(GK):
                    cols = slice(k * P, (k + 1) * P)
                    ch = 2 * KK + g * GK + k
                    nc.scalar.activation(far_m[:, cols], bank[2][:, cols], ACT.Sigmoid, bias=boff_all[:, ch:ch + 1])
                act.wait_ge(s("far_coords"), n + 1)
                nc.scalar.activation(far_px, far_px, ACT.Abs).then_inc(s("far_px_abs"), 1)
                act.wait_ge(s("far_px_abs"), n + 1)
                nc.scalar.activation(far_hx, far_px, ACT.Relu, bias=SA, scale=-SA).then_inc(s("far_hat"), 1)
                with act.Fori(0, NB) as q:
                    t = n * NB + q
                    act.wait_ge(s("far_a"), t + OPEN)
                    nc.scalar.activation(far_t, far_py, ACT.Abs, bias=far_rows[:, ds(MB * m + o % MB + NB - 1 - q, 1)]
                                         ).then_inc(s("far_py_abs"), 1)
                    act.wait_ge(s("far_py_abs"), t + 1)
                    nc.scalar.activation(far_t, far_t, ACT.Relu, bias=1.0, scale=-1.0).then_inc(s("far_hy"), 1)

            def far_macro(m):
                for o in range(NO):
                    far_group(m, (far * NM + m) * NO + o, o)
                    if o % MB == 0:
                        act.wait_ge(s(f"conv{o // MB}"), i * NM + m + OPEN)
                    back((i * NM + m) * NO + o, o)

            def macro(m, last):
                base = (i * NM + m) * NO
                for o in range(NO):
                    if o + 2 < NO or not last:
                        if o + 2 >= 3:
                            act.wait_ge(s("sampled"), base + o)
                        front((near * NM + m) * NO + o + 2, o + 2)
                    if o % MB == 0:
                        act.wait_ge(s(f"conv{o // MB}"), i * NM + m + OPEN)
                    back(base + o, o)

            act.wait_ge(s("r_done"), (i + 1) * NC + OPEN)
            is_far, far, near = which_path(act, i, counts)
            with act.If(is_far):
                with act.Fori(0, NM) as m:
                    far_macro(m)
                act.reg_add(counts[0], counts[0], 1)
            with act.Else():
                for o in range(2):
                    front(near * (NM * NO) + o, o)
                with act.Fori(0, NM - 1) as m:
                    macro(m, False)
                macro(NM - 1, True)
                act.reg_add(counts[1], counts[1], 1)

            act.wait_ge(s("gn_var1"), i + 1)
            nc.scalar.activation(gst[:, 5, :], gst[:, 4, :], ACT.Sqrt).then_inc(s("gn_sqrt1"), 1)
            with act.Fori(0, NC // 2) as c:
                for u in range(2):
                    act.wait_ge(s("an_ready"), i * (2 * NC) + 2 * c + u + 1)
                    act.wait_ge(s(f"sq_used{u}"), i * (NC // 2) + c + OPEN)
                    nc.scalar.activation(sq[u], an[u], ACT.Square).then_inc(s(f"sq_ready{u}"), 1)
            act.wait_ge(s("norm_sums"), i + 1)
            nc.scalar.activation(c1[:, 0, :], bank[2][:, 0:NB], ACT.Sqrt).then_inc(s("norm_sqrt"), 1)
            act.wait_ge(s("rnorm"), i + 1)
            stand(act)
            with act.Fori(0, NC // 2) as c:
                for u in range(2):
                    n = i * NC + 2 * c + u
                    act.wait_ge(s(f"qkv_ready{u}"), i * (NC // 2) + c + 1 + OPEN)
                    act.wait_ge(s(f"q_t{u}"), i * (NC // 2) + c + OPEN)
                    for t in range(4):
                        ti = (2 * c + u) * 4 + t
                        r = c1[:, 2, ds(ti, 1)]
                        b = bank[t]
                        nc.scalar.activation(qs[u][:, t * HID:(t + 1) * HID], b[:, 0:HID], ACT.Copy, scale=r)
                        nc.scalar.activation(kt[:, ds(ti, 1), :].rearrange("p t d -> p (t d)"), b[:, HID:2 * HID], ACT.Copy, scale=r)
                        ins = nc.scalar.activation(vt[:, ds(ti, 1), 0:HID].rearrange("p t d -> p (t d)"), b[:, 2 * HID:3 * HID], ACT.Copy, scale=r)
                    ins.then_inc(s("qkv_copied"), 1)
                    act.wait_ge(s("q_shifted"), n + 1)
                    nc.scalar.activation(qe[u], qs[u], ACT.Exp).then_inc(s("q_exp"), 1)
                    act.wait_ge(s(f"q_t{u}"), i * (NC // 2) + c + 1 + OPEN)
                    nc.scalar.activation(q_soft[:, ds((2 * c + u) * CH, CH)], bank[5][:, :], ACT.Copy).then_inc(s("q_t_copied"), 1)
            act.wait_ge(s("kdiag_ready"), i + 1)
            nc.scalar.activation(ekm[:, 0:MEM], memk[:, :], ACT.Exp, bias=c2[:, 6, 3:4]).then_inc(s("ekm_ready"), 1)
            with act.Fori(0, NC // 2) as c:
                for u in range(2):
                    act.wait_ge(s("k_shifted"), i * NC + 2 * c + u + 1)
                    act.wait_ge(s(f"ctx_done{u}"), i * (NC // 2) + c + OPEN)
                    nc.scalar.activation(ek[u], ekx[u], ACT.Exp).then_inc(s(f"ek_ready{u}"), 1)
            with act.Fori(0, NC // 2) as c:
                for u in range(2):
                    n = i * NC + 2 * c + u
                    act.wait_ge(s("o_psum"), n + 1)
                    act.wait_ge(s("y_ready"), i * NC + 2 * c + u // 2 + OPEN)
                    for h in range(NH):
                        if h == 0 and u == 0:
                            pass
                        ins = nc.scalar.activation(an[u][:, h, :], bank[2 * u + h][:, :], ACT.Identity, bias=bout[:, h:h + 1])
                    ins.then_inc(s("o_copied"), 1)
                    act.wait_ge(s("o_copied"), n + 1 + OPEN)
                    nc.scalar.activation(sq[u], an[u], ACT.Square).then_inc(s("osq_ready"), 1)
                    act.wait_ge(s("osum_ready"), n + 1)
                    nc.scalar.activation(c1[:, 3, 4 * u:4 * u + 4], bank[5][:, 0:4], ACT.Sqrt,
                                         scale=1.0 / C).then_inc(s("o_sqrt"), 1)

    @block.tensor
    def _(pe):
        mm = nc.tensor.matmul
        pe.wait_ge(s("const_in"), 16 * N_CONST)
        pe.wait_ge(s("wc_split"), 1)
        for e in range(NWT):
            if e >= 2:
                pe.wait_ge(s("wt_copied"), e - 1)
            b = bank[e % 2][:, :].bitcast(f16)
            for n in range(8):
                k, half, part, oh = (2 * e + n // 4) // NH, (2 * e + n // 4) % NH, n // 2 % 2, n % 2
                c0 = k * C + half * P
                ins = nc.tensor.transpose(b[:, n * P:(n + 1) * P], wc_hl[part][:, oh, c0:c0 + P], ident16[:, :])
            ins.then_inc(s("wt_ready"), 1)
        pe.wait_ge(s("wo_split"), 1)
        for e in range(NWO):
            pe.wait_ge(s("wt_copied"), NWT + e - 1)
            b = bank[(NWT + e) % 2][:, :].bitcast(f16)
            for n in range(min(8, 2 * KK * NH - 8 * e)):
                kh, part = (8 * e + n) // 2, n % 2
                tap, half = kh // NH, kh % NH
                c0 = tap * C + half * P
                ins = nc.tensor.transpose(b[:, n * 32:(n + 1) * 32], wo_hl[part][0:32, c0:c0 + P], ident16[0:32, 0:32])
            ins.then_inc(s("wt_ready"), 1)
        pe.wait_ge(s("wa_in"), 32)
        for n in range(9):
            if n >= 2:
                pe.wait_ge(s("wa_copied"), n - 1)
            if n < 6:
                src = wq_raw[:, n // NH, (n % NH) * P:(n % NH + 1) * P]
            elif n < 8:
                src = wu_raw[:, n - 6, :]
            else:
                src = memv_raw[:, :]
            nc.tensor.transpose(bank[2 + n % 2][0:src.shape[1], 0:P], src, ident32[:, :]).then_inc(s("wa_ready"), 1)
        pe.wait_ge(s("wa_copied"), 8)
        mm(bank[3][:, 0:1], spread[0:27, 0, :], boff[:, :], start=True, stop=True)
        mm(bank[3][:, 1:2], spread[0:27, 1, :], boff[:, :], start=True, stop=True).then_inc(s("bias_rows"), 1)

        counts = path_counts(pe)
        PASSES = [(0, 0), (0, 1), (1, 0)]

        with pe.Fori(0, ni) as i:
            pe.wait_ge(s("gn_sums0"), i + 1)
            mm(bank[0][:, 0:4], group_mean[:, :], gst[:, 0:2, :].rearrange("p a h -> p (a h)"), start=True,
               stop=True).then_inc(s("gn_means0"), 1)
            pe.wait_ge(s("xn_lo"), (i + 1) * 8)
            stand(pe)
            with pe.Fori(0, NB // 4) as t:
                for u in range(2):
                    pe.wait_ge(s(f"xt_copied{u}"), i * (NB // 4) + t + OPEN)
                    b = bank[u][:, :].bitcast(f16)
                    for n in range(8):
                        m, part, half = n // 4, n // 2 % 2, n % 2
                        src = xp[:, part, half, ds((8 * t + 4 * u + 2 * m + 1) * W, P)]
                        ins = nc.tensor.transpose(b[:, n * P:(n + 1) * P], src, ident16[:, :])
                    ins.then_inc(s(f"xt_ready{u}"), 1)
            for c in range(NC):
                if c >= 2:
                    pe.wait_ge(s("off_copied"), i * NC + c - 1)
                for r in range(-(-KK * NH // 4)):
                    for a, b in PASSES:
                        for j in range(4):
                            n = 4 * r + j
                            if n < KK * NH:
                                tap, half = n // NH, n % NH
                                y0, dx = c * RC + tap // 3, tap % 3 - 1
                                a0, a1 = max(0, -dx), W - max(0, dx)
                                dst = bank[2 + c % 2][32 * j:32 * j + 32, :].rearrange("p (r w) -> p r w", w=W)
                                src = xp[:, b, half, y0 * W:(y0 + RC) * W].rearrange("p (r w) -> p r w", w=W)
                                ins = mm(dst[:, :, a0:a1], wofft[:, n, a, :], src[:, :, a0 + dx:a1 + dx], start=n < 4 and (a, b) == (0, 0),
                                         stop=n + 4 >= KK * NH and (a, b) == PASSES[-1], skip_group_check=True)
                ins.then_inc(s("off_ready"), 1)
            pe.wait_ge(s("off_copied"), (i + 1) * NC)
            stand(pe)
            with pe.Fori(0, NC) as c:
                pe.wait_ge(s("r_done"), i * NC + c + OPEN)
                for n in range(4):
                    for t in range(NT):
                        a, e = WIN[t]
                        src = offs[:, ds((c * RC + 4 * (n % 2)) * W, 4 * W)].rearrange("p (r w) -> p r w", w=W)[:, :, a:e]
                        dst = bank[4 + n][:, 0:4 * WW].rearrange("p (r w) -> p r w", w=WW)[:, :, WOFF[t]:WOFF[t] + e - a]
                        ins = mm(dst, spread[:, n // 2, :], src, start=True, stop=True)
                ins.then_inc(s("r_ready"), 1)

            def front(f, m, o):
                u, g = o % MB, (o // MB) % NG
                row = PR * (MB * m + u) if o < NO else PR * (MB * m + MB + u)
                pe.wait_ge(s("hx_read"), f + OPEN)
                for k in range(GK):
                    ins = mm(bank[BANK_HX][:, k * PR * WW:(k + 1) * PR * WW], pick_x[:, g * GK + k, :],
                             dxw[:, ds(row * WW, PR * WW)], start=True, stop=True)
                ins.then_inc(s("hx_ready"), 1)
                if not isinstance(o, int) or o >= 2:
                    pe.wait_ge(s("a_full"), f - 1)
                for k in range(GK):
                    for y in range(PR):
                        n = k * PR + y
                        ins = mm(bank[BANK_HY[o % 2]][:, n * WW:(n + 1) * WW], pick_y[:, g * GK + k, y, :],
                                 vhat[:, ds((row + y) * WW, WW)], start=True, stop=True)
                ins.then_inc(s("hy_ready"), 1)

            def sample(f, Gm, G, o):
                u, g = o % MB, o // MB
                pe.wait_ge(s("a_lo"), f + 1)
                pe.wait_ge(s("s_lo"), G * NO + max(0, o - 1) + OPEN)
                if g == 0:
                    pe.wait_ge(s(f"xt_in{u}"), (Gm + 1) * (16 * NT))
                for h in range(NH):
                    dst = bank[BANK_S[o % 2] + h][:, 0:GK * P].rearrange("p (k n) -> p k n", n=W)
                    for t in range(NT):
                        a0, a1 = WIN[t]
                        for a, b in PASSES:
                            src = a_hl[o % 3][b].rearrange("p (k n) -> p k n", n=WW)[:, :, WOFF[t]:WOFF[t] + a1 - a0]
                            ins = mm(dst[:, :, a0:a1], xt[:, u, t, a * C + h * P:a * C + (h + 1) * P], src,
                                     start=t == 0 and (a, b) == (0, 0), stop=t == NT - 1 and (a, b) == PASSES[-1],
                                     skip_group_check=True)
                ins.then_inc(s("sampled"), 1)

            def conv(G, g, oh):
                if oh == 0:
                    pe.wait_ge(s("s_lo"), G * NO + MB * (g + 1) + OPEN)
                    if g == 0:
                        pe.wait_ge(s("x1_ready"), G + OPEN)
                for k in range(g * GK, (g + 1) * GK):
                    for half in range(NH):
                        for a, b in PASSES:
                            first = k == 0 and half == 0 and (a, b) == (0, 0)
                            final = k == KK - 1 and half == NH - 1 and (a, b) == PASSES[-1]
                            ins = mm(bank[BANK_O][:, oh * MP:(oh + 1) * MP], wt[:, k * NH + half, a, oh * P:(oh + 1) * P],
                                     S[:, b, half, k, :], start=first and oh == 0, stop=final, skip_group_check=True)
                            if g == NG - 2 and (k, half, a, b) == (g * GK, 0, 0, 0):
                                ins.then_inc(s(f"xt_used{oh}"), 1)
                if oh == 1:
                    ins.then_inc(s(f"conv{g}"), 1)

            def macro(m, last):
                G, Gm = i * NM + m, near * NM + m
                for o in range(NO):
                    if o + 2 < NO or not last:
                        front(Gm * NO + o + 2, m, o + 2)
                    sample(Gm * NO + o, Gm, G, o)
                    if o >= 2:
                        conv(G, o // 2 - 1, o % 2)
                for oh in range(2):
                    conv(G, NG - 1, oh)

            pe.wait_ge(s("r_done"), (i + 1) * NC + OPEN)
            def far_group(m, n, G, o):
                u, g = o % MB, o // MB
                for k in range(GK):
                    for b in range(3):
                        ch = b * KK + g * GK + k
                        ins = mm(bank[b][:, k * P:(k + 1) * P], of_channel[:, ch:ch + 1].to_broadcast([P, P]),
                                 offs[:, ds((MB * m + u) * P, P)], start=True, stop=True)
                ins.then_inc(s("far_spread"), 1)
                pe.wait_ge(s("s_lo"), G * NO + max(0, o - 1) + OPEN)
                dst = [bank[BANK_S[o % 2] + h][:, 0:GK * P] for h in range(NH)]
                some = pick_y[:, 0:2, :, :].rearrange("p a b c -> p (a b c)")[:, 0:GK * P]
                for h in range(NH):
                    mm(dst[h], zero16[:, :], some, start=True, stop=False, skip_group_check=True)
                with pe.Fori(0, NB) as q:
                    t = n * NB + q
                    pe.wait_ge(s("far_in"), (t + 1) * 16)
                    pe.wait_ge(s("far_a_lo"), t + 1)
                    for h in range(NH):
                        for a, b in PASSES:
                            ins = mm(dst[h], xt[:, 0, 0, a * C + h * P:a * C + (h + 1) * P], far_hl[b], start=False,
                                     stop=False, skip_group_check=True)
                    ins.then_inc(s("far_used"), 1)
                for h in range(NH):
                    ins = mm(dst[h], zero16[:, :], some, start=False, stop=True, skip_group_check=True)
                ins.then_inc(s("sampled"), 1)

            def far_macro(m):
                G = i * NM + m
                for o in range(NO):
                    far_group(m, (far * NM + m) * NO + o, G, o)
                for g in range(NG):
                    for oh in range(2):
                        conv(G, g, oh)

            is_far, far, near = which_path(pe, i, counts)
            with pe.If(is_far):
                with pe.Fori(0, NM) as m:
                    far_macro(m)
                pe.reg_add(counts[0], counts[0], 1)
            with pe.Else():
                for o in range(2):
                    front(near * (NM * NO) + o, 0, o)
                with pe.Fori(0, NM - 1) as m:
                    macro(m, False)
                macro(NM - 1, True)
                pe.reg_add(counts[1], counts[1], 1)

            pe.wait_ge(s("gn_sums1"), i + 1)
            mm(bank[0][:, 0:4], group_mean[:, :], gst[:, 0:2, :].rearrange("p a h -> p (a h)"), start=True,
               stop=True).then_inc(s("gn_means1"), 1)
            with pe.Fori(0, NC // 2) as c:
                for u in range(2):
                    pe.wait_ge(s(f"sq_ready{u}"), i * (NC // 2) + c + 1 + OPEN)
                    for t in range(4):
                        for h in range(NH):
                            ins = mm(bank[2][:, ds((2 * c + u) * 4 + t, 1)], sq[u][:, h, t * P:(t + 1) * P],
                                     ones32[:, 0:1], start=h == 0, stop=h == NH - 1)
                    ins.then_inc(s(f"sq_used{u}"), 1)
            pe.wait_ge(s("gn_sqrt1"), i + 1)
            mm(bank[2][:, NB:NB + 1], ones32[:, :], ones32[:, 0:1], start=True, stop=True).then_inc(s("norm_sums"), 1)
            pe.wait_ge(s("norm_sqrt"), i + 1)
            stand(pe)
            with pe.Fori(0, NC // 2) as c:
                for u in range(2):
                    n = i * NC + 2 * c + u
                    pe.wait_ge(s("an_ready"), i * (2 * NC) + NC + 2 * c + u + 1)
                    pe.wait_ge(s("qkv_copied"), n + OPEN)
                    for t in range(4):
                        for h in range(NH):
                            ins = mm(bank[t][:, 0:3 * HID], an[u][:, h, t * P:(t + 1) * P], wqkvt[:, h, :],
                                     start=h == 0, stop=h == NH - 1)
                    ins.then_inc(s(f"qkv_ready{u}"), 1)
                    pe.wait_ge(s("q_ready"), n + 1)
                    pe.wait_ge(s("q_t_copied"), n + OPEN)
                    for t in range(4):
                        ins = nc.tensor.transpose(bank[5][:, t * P:(t + 1) * P], qe[u][:, t * P:(t + 1) * P], ident32[:, :])
                    ins.then_inc(s(f"q_t{u}"), 1)
            pe.wait_ge(s("kred_ready"), i + 1)
            nc.tensor.transpose(bank[6][:, 0:P], kred, ident32[:, :]).then_inc(s("kred_t"), 1)
            pe.wait_ge(s("kdiag_ready"), i + 1)
            mm(bank[6][:, 0:P], ones32[:, :], kdiag, start=True, stop=True).then_inc(s("kmb_ready"), 1)
            pe.wait_ge(s("ekm_ready"), i + 1)
            pe.wait_ge(s("kmb_copied"), i + 1)
            nc.tensor.transpose(bank[6][0:MEM, 0:P], ekm[:, 0:MEM], ident32[:, :]).then_inc(s("ekm_t"), 1)
            def context(u, tiles, start):
                for t in range(4):
                    ins = mm(bank[7][:, 0:HID + 1], ek[u][:, t * P:(t + 1) * P], tiles(t), start=start and t == 0,
                             stop=False, skip_group_check=True)
                ins.then_inc(s(f"ctx_done{u}"), 1)
            pe.wait_ge(s("v_ones"), i + 1)
            def vtile(ti):
                return vt[:, ds(ti, 1), :].rearrange("p t e -> p (t e)")
            for u in range(2):
                pe.wait_ge(s(f"ek_ready{u}"), i * (NC // 2) + 1 + OPEN)
                context(u, lambda t, u=u: vtile(4 * u + t), u == 0)
            with pe.Fori(1, NC // 2) as c:
                for u in range(2):
                    pe.wait_ge(s(f"ek_ready{u}"), i * (NC // 2) + c + 1 + OPEN)
                    context(u, lambda t, u=u: vtile((2 * c + u) * 4 + t), False)
            pe.wait_ge(s("ekmt_ready"), i + 1)
            mm(bank[7][:, 0:HID + 1], ekmt[0:MEM, :], memv[:, :], start=False, stop=True,
               skip_group_check=True).then_inc(s("ctx_ready"), 1)
            pe.wait_ge(s("ctxn_ready"), i + 1)
            nc.tensor.transpose(bank[6][:, 0:P], ctxn, ident32[:, :]).then_inc(s("ctx_t"), 1)
            pe.wait_ge(s("ctxt_ready"), i + 1)
            mm(bank[6][:, 0:C], ctxt, woutt[:, :], start=True, stop=True).then_inc(s("m2_psum"), 1)
            pe.wait_ge(s("m2_ready"), i + 1)
            pe.wait_ge(s("q_t_copied"), (i + 1) * NC + OPEN)
            pe.wait_ge(s("qkv_copied"), (i + 1) * NC + OPEN)
            stand(pe)
            with pe.Fori(0, NC // 2) as c:
                for u in range(2):
                    n = i * NC + 2 * c + u
                    pe.wait_ge(s("o_copied"), n + OPEN)
                    for h in range(NH):
                        ins = mm(bank[2 * u + h][:, :], m2[:, h * P:(h + 1) * P], q_soft[:, ds((2 * c + u) * CH, CH)],
                                 start=True, stop=True)
                    ins.then_inc(s("o_psum"), 1)
                    pe.wait_ge(s("osq_ready"), n + 1)
                    pe.wait_ge(s("o_sqrt"), n + OPEN)
                    for t in range(4):
                        for h in range(NH):
                            ins = mm(bank[5][:, t:t + 1], sq[u][:, h, t * P:(t + 1) * P], ones32[:, 0:1],
                                     start=h == 0, stop=h == NH - 1)
                    ins.then_inc(s("osum_ready"), 1)
                    pe.wait_ge(s("odiag_ready"), n + 1)
                    pe.wait_ge(s("o_scaled"), n + OPEN)
                    mm(bank[4][:, :], ones32[:, :], odiag[u], start=True, stop=True).then_inc(s("rb_ready"), 1)


_INS = ["x", "L0_conv_w_off", "L0_conv_b_off", "L0_conv_w_conv", "L1_conv_g1", "L1_conv_mem_kv", "L1_conv_w_qkv",
        "L1_conv_w_out", "L1_conv_b_out", "L1_conv_g2"]


def build_program(nc, shapes, ni):
    dram = {}
    for name, (shape, dt) in shapes.items():
        dram[name] = nc.dram_tensor(f"in_{name}_dram", shape, dt, kind="ExternalInput").ap()
    dram["x_v"] = dram["x"].rearrange("n (h p) r w -> n h p (r w)", p=P)
    y = nc.dram_tensor("out_0_dram", (ni, C, H, W), mybir.dt.float32, kind="ExternalOutput").ap()
    with ExitStack() as ctx:
        deform_attention(nc, ctx, ni, dram, y.rearrange("n (h p) r w -> n h p (r w)", p=P))


def kernel(**inputs):
    import concourse.bacc as _bacc
    from concourse import mybir as _mybir
    from concourse.bass_utils import run_bass_kernel_spmd as _run

    nc = _bacc.Bacc("TRN2", target_bir_lowering=False, num_devices=1)
    arrays, shapes = {}, {}
    for name, a in [(n, inputs[n]) for n in _INS] + list(tables().items()):
        a = np.ascontiguousarray(a)
        arrays[f"in_{name}_dram"] = a
        shapes[name] = (a.shape, _mybir.dt.from_np(a.dtype))
    ni = inputs["x"].shape[0]
    build_program(nc, shapes, ni)
    r = _run(nc, [arrays], core_ids=[0])
    return r.results[0]["out_0_dram"]
```

```python
from contextlib import ExitStack

import concourse.bass as bass
import numpy as np
from concourse import mybir


NI, C, H, W = 8, 256, 64, 64
HW = H * W
P = 128
NH = C // P
KK = 9
R = 3
QR, QC = 8, 16
NT = W // QC
PR = QR - 2 * R
WIN = [(max(0, QC * t - R), min(W, QC * (t + 1) + R)) for t in range(NT)]
WOFF = [sum(b - a for a, b in WIN[:t]) for t in range(NT)]
WW = sum(b - a for a, b in WIN)
NE = 2 * R + 1
NG = 3
GK = KK // NG
GW = GK * PR * WW
NB = H // PR
MB = 2
NM = NB // MB
MP = MB * PR * W
NO = MB * NG
XR = H + 2 * R
PADR = H + 2
SX, SA = 16.0, 16.0
SW = 256.0
HEADS, DH = 4, 32
HID = HEADS * DH
MEM = 4
CH = 512
NC = HW // CH
RC = CH // W
EPS = 1e-5


def tables():
    p = np.arange(P)
    t = {}
    t["ident16"] = np.eye(P, dtype=np.float16)
    t["ident32"] = np.eye(P, dtype=np.float32)
    t["ones32"] = np.ones((P, P), np.float32)
    per = C // 32
    t["group_mean"] = ((p[:, None] // per == p[None] // per) / per).astype(np.float32)
    t["head_mask"] = (p[:, None] // DH == p[None] // DH).astype(np.float32)
    sel = np.zeros((P, 2, P), np.float32)
    for j in range(4):
        for k in range(KK):
            for e in range(NE):
                sel[32 * j + k, 0, k * NE + e] = 1
                sel[32 * j + 2 * KK + k, 1, k * NE + e] = 1
            sel[32 * j + KK + k, 0, 64 + k] = 1
            sel[32 * j + k, 0, 96 + k] = 1
    t["spread"] = sel
    sy = np.zeros((P, KK, PR, P), np.float16)
    for k in range(KK):
        for y in range(PR):
            for q in range(P):
                e = q // QC - y
                if 0 <= e < NE:
                    sy[k * NE + e, k, y, q] = 1
                    sy[64 + k * NE + e, k, y, q] = 1
    t["pick_y"] = sy
    sx = np.zeros((P, KK, P), np.float16)
    for k in range(KK):
        sx[64 + k, k] = 1
        sx[96 + k, k] = 1
        sx[0, k] = 1
    t["pick_x"] = sx
    t["window_column"] = np.tile(
        np.concatenate([SX * (np.arange(a, b) - QC * i) for i, (a, b) in enumerate(WIN)]), H
    ).astype(np.float16)[None]
    t["of_channel"] = (p[:, None] % 32 == np.arange(32)[None]).astype(np.float32)
    px = np.arange(PR * W)
    t["far_xy"] = np.stack([px[None] // W - p[:, None] // W, px[None] % W - p[:, None] % W], 1).astype(np.float32)
    t["far_rows"] = np.tile(float(PR) * (np.arange(2 * NB) - (NB - 1)), (P, 1)).astype(np.float32)
    small = np.zeros((P, 3), np.float32)
    small[:, 0] = -(p % QC)
    small[: KK * NE, 1] = -(p[: KK * NE] % NE - R)
    small[:, 2] = EPS
    t["small"] = small
    return t


TABLES = ["ident16", "ident32", "ones32", "group_mean", "head_mask", "spread", "pick_y", "pick_x",
          "window_column", "small", "of_channel", "far_xy", "far_rows"]


class Count:

    def __init__(self, eng, sem):
        self.eng, self.sem, self.base, self.n = eng, sem, 0, 0

    def at(self, base):
        self.base, self.n = base, 0

    def inc(self, ins):
        ins.then_inc(self.sem, 1)
        self.n += 1
        return self

    def wait(self):
        self.eng.wait_ge(self.sem, self.base + self.n)


def deform_attention(nc, ctx, ni, dram, out):
    f32, f16, i32 = mybir.dt.float32, mybir.dt.float16, mybir.dt.int32
    ALU = mybir.AluOpType
    ACT = mybir.ActivationFunctionType
    X = mybir.AxisListType.X
    ds = bass.ds

    def sb(name, shape, dt):
        return ctx.enter_context(nc.sbuf_tensor(name, shape, dt))

    def sem(name):
        return ctx.enter_context(nc.semaphore(name))

    x = sb("x", [P, NH, HW], f32)
    arena_x = sb("arena_x", [P, NH * PADR * W], f32)
    xp = arena_x[:, :].bitcast(f16).rearrange("p (s h n) -> p s h n", s=2, h=NH)
    kv = arena_x[:, 0:NB * (2 * HID + 1)].rearrange("p (t e) -> p t e", e=2 * HID + 1)
    offs = sb("offs", [P, HW], f32)
    q_soft = offs[:, :]
    vhat = sb("vhat", [P, H * WW], f16)
    dxw = sb("dxw", [P, H * WW], f16)
    wt = sb("wt", [P, KK * NH, 2, C], f16)
    wofft = sb("wofft", [P, KK * NH, 2, 32], f16)
    wqkvt = sb("wqkvt", [P, NH, 3 * HID], f32)
    woutt = sb("woutt", [P, C], f32)
    ident16 = sb("ident16", [P, P], f16)
    ident32 = sb("ident32", [P, P], f32)
    ones32 = sb("ones32", [P, P], f32)
    group_mean = sb("group_mean", [P, P], f32)
    head_mask = sb("head_mask", [P, P], f32)
    spread = sb("spread", [P, 2, P], f32)
    pick_y = sb("pick_y", [P, KK, PR, P], f16)
    pick_x = sb("pick_x", [P, KK, P], f16)
    small = sb("small", [P, 3], f32)
    of_channel = sb("of_channel", [P, 32], f32)
    far_xy = sb("far_xy", [P, 2, PR * W], f32)
    far_rows = sb("far_rows", [P, 2 * NB], f32)
    boff_all = sb("boff_all", [P, 3 * KK], f32)
    boff_half = sb("boff_half", [P, 3 * KK], f32)
    zero16 = sb("zero16", [P, P], f16)
    far_flag = sb("far_flag", [P, 1], i32)
    boff = sb("boff", [3 * KK, 1], f32)
    bias_r = sb("bias_r", [P, 2], f32)
    wmax = sb("wmax", [P, 2, 4], f32)
    wall = sb("wall", [P, 2, 4], f32)
    g1 = sb("g1", [P, NH], f32)
    g2 = sb("g2", [P, NH], f32)
    bout = sb("bout", [P, NH], f32)
    memk = sb("memk", [P, MEM], f32)
    memv = sb("memv", [MEM, HID + 1], f32)
    memv_raw = sb("memv_raw", [P, MEM], f32)
    st = [sb(f"stats{n}", [P, NH, NM, 6], f32) for n in range(2)]
    mv = sb("mv", [P, NH, 2], f32)
    gst = sb("gst", [P, 12, NH], f32)
    far_max = sb("far_max", [P, NC], f32)
    far_red = sb("far_red", [P, 4], f32)
    c1 = sb("c1", [P, 6, NB], f32)
    c2 = sb("c2", [P, 8, 16], f32)
    work = sb("work", [P, 10944], f32)

    def carve(at, n, dt):
        m = n if dt == f32 else n // 2
        v = work[:, at:at + m]
        return v if dt == f32 else v.bitcast(dt)

    xt = carve(0, 2 * NT * 512, f16).rearrange("p (u t c) -> p u t c", u=2, t=NT)
    S = carve(2048, 2 * NH * KK * MP, f16).rearrange("p (s h k n) -> p s h k n", s=2, h=NH, k=KK)
    t_abs = [carve(6656 + 496 * n, GW, f32) for n in range(1)]
    hat_x = [carve(7152 + 496 * n, GW, f32) for n in range(2)]
    a_full = [carve(8144 + 496 * n, GW, f32) for n in range(2)]
    a_hl = [[carve(9136 + 248 * (2 * n + s), GW, f16) for s in range(2)] for n in range(3)]
    far_py, far_px, far_m, far_hx, far_t, far_a = (carve(6656 + GK * P * n, GK * P, f32) for n in range(6))
    far_hl = [carve(6656 + 6 * GK * P + GK * P // 2 * n, GK * P, f16) for n in range(2)]
    xn_tmp = [carve(1024 * n, 1024, f32) for n in range(2)]
    stage = [carve(2048 + 512 * n, 1024, f16) for n in range(4)]
    r_abs, r_hat, r_sig, r_v, r_d = (carve(4096 + 2 * 328 * n, 656, f32) for n in range(5))
    an = [carve(at, 1024, f32).rearrange("p (h n) -> p h n", h=NH) for at in (0, 1024, 4096)]
    sq = [carve(2048 + 1024 * n, 1024, f32).rearrange("p (h n) -> p h n", h=NH) for n in range(2)]
    qs = [carve(4096 + 512 * n, 512, f32) for n in range(2)]
    qe = [carve(5120 + 512 * n, 512, f32) for n in range(2)]
    ek = [carve(6144 + 512 * n, 512, f32) for n in range(2)]
    ekx = [carve(7168 + 512 * n, 512, f32) for n in range(2)]
    kmx = carve(8192, 512, f32)
    kmb = carve(8704, 128, f32)
    kred = carve(8832, 128, f32)
    kdiag = carve(8960, 128, f32)
    ctxn = carve(9088, 128, f32)
    ctxt = carve(9216, 128, f32)
    m2 = carve(9344, 256, f32)
    ekm = carve(9600, 8, f32)
    ekmt = carve(9616, 128, f32)
    odiag = [carve(9744 + 512 * n, 512, f32) for n in range(2)]
    wc_raw = x[:, :, :].rearrange("p h n -> p (h n)")[:, 0:NH * KK * C].rearrange("p (h n) -> p h n", h=NH)
    wc_hl = [arena_x[:, 4608 // 2 * s:4608 // 2 * (s + 1)].bitcast(f16).rearrange("p (h n) -> p h n", h=NH)
             for s in range(2)]
    wo_raw = x[:, :, :].rearrange("p h n -> p (h n)")[:, 4608:4608 + KK * C]
    wo_hl = [arena_x[:, 4608 + 1152 * s:4608 + 1152 * (s + 1)].bitcast(f16) for s in range(2)]
    wq_raw = work[:, 0:3 * C].rearrange("p (a c) -> p a c", a=3)
    wu_raw = work[:, 1024:1024 + NH * HID].rearrange("p (a c) -> p a c", a=NH)

    bank = [ctx.enter_context(nc.psum_tensor(f"bank{n}", [P, 512], f32)) for n in range(8)]
    xtd = nc.dram_tensor("xt_scratch", (XR, W, 2 * C), f16, kind="Internal").ap()

    S_ = {}

    def s(name):
        if name not in S_:
            S_[name] = sem(name)
        return S_[name]

    OPEN = 1
    OPENED = [*(f"xt_copied{u}" for u in range(4)), *(f"xt_out{u}" for u in range(4)), "xt_used0", "xt_used1",
              "far_used", "y_ready", "r_done", "sq_ready0", "sq_ready1", "ek_ready0", "ek_ready1", "conv0", "conv1",
              "conv2", "s_lo", "x1_ready", "hx_read", "far_a", "sq_used0", "sq_used1", "ctx_done0", "ctx_done1"]

    block = ctx.enter_context(nc.Block())
    BANK_HX, BANK_HY, BANK_S, BANK_O = 0, (1, 2), (3, 5), 7
    NWT = KK * NH * 4 // 8
    N_CONST = 23
    NWO = 5

    def stand(eng):
        eng.sem_inc(s(f"stood_{eng.engine.name}"), 1)

    def path_counts(eng):
        regs = [eng.alloc_register(name) for name in ("far_images", "near_images")]
        for reg in regs:
            eng.reg_mov(reg, 0)
        return regs

    def which_path(eng, i, counts):
        eng.wait_ge(s("far_flag_ready"), i + 1)
        stand(eng)
        flag = eng.value_load(far_flag[0:1, 0:1], min_val=0, max_val=1)
        return flag > 0, *(eng.snap(reg, min_val=0, max_val=ni) for reg in counts)

    @block.sync
    def _(sp):
        for name, tile in (("ident16", ident16), ("ident32", ident32), ("ones32", ones32),
                           ("group_mean", group_mean), ("head_mask", head_mask), ("spread", spread),
                           ("pick_y", pick_y), ("pick_x", pick_x), ("small", small), ("of_channel", of_channel),
                           ("far_xy", far_xy), ("far_rows", far_rows)):
            full = tile[tuple(slice(None) for _ in tile.shape)]
            sp.dma_start(full, dram[name]).then_inc(s("const_in"), 16)
        sp.dma_start(boff_all[:, :], dram["L0_conv_b_off"].rearrange("(o n) -> o n", o=1).to_broadcast([P, 3 * KK])
                     ).then_inc(s("const_in"), 16)
        sp.dma_start(wc_raw, dram["L0_conv_w_conv"].rearrange("(h p) n -> p h n", p=P)).then_inc(s("wc_in"), 16)
        sp.wait_ge(s("zeroed"), 1)
        sp.dma_start(wo_raw[0:3 * KK, :], dram["L0_conv_w_off"].rearrange("o c a b -> o (c a b)")).then_inc(s("wo_in"), 16)
        sp.dma_start(wq_raw, dram["L1_conv_w_qkv"].rearrange("(a p) c -> p a c", p=P)).then_inc(s("wa_in"), 16)
        sp.dma_start(wu_raw, dram["L1_conv_w_out"].rearrange("(a p) c -> p a c", p=P)).then_inc(s("wa_in"), 16)
        sp.dma_start(boff[:, :], dram["L0_conv_b_off"].rearrange("(p n) -> p n", n=1)).then_inc(s("const_in"), 16)
        for tile, name in ((g1, "L1_conv_g1"), (g2, "L1_conv_g2")):
            for h in range(NH):
                sp.dma_start(tile[:, h:h + 1], dram[name][0, h * P:(h + 1) * P, 0, :]).then_inc(s("const_in"), 16)
        for h in range(NH):
            sp.dma_start(bout[:, h:h + 1], dram["L1_conv_b_out"][h * P:(h + 1) * P].rearrange("(p n) -> p n", n=1)
                         ).then_inc(s("const_in"), 16)
        mkv = dram["L1_conv_mem_kv"].rearrange("a h d m -> a (h d) m")
        sp.dma_start(memk[:, :], mkv[0]).then_inc(s("const_in"), 16)
        sp.dma_start(memv_raw[:, :], mkv[1]).then_inc(s("const_in"), 16)
        for r0 in (0, XR - R):
            sp.dma_start(xtd[r0:r0 + R, :, :].rearrange("r (a w) c -> (r a) (w c)", a=32),
                         vhat[0:R * 32, 0:2 * W * C // 32]).then_inc(s("zero_rows"), 16)
        sp.dma_start(dxw[0:1, :], dram["window_column"]).then_inc(s("const_in"), 16)

        def load(i, c):
            sp.dma_start(x[:, :, c * CH:(c + 1) * CH], dram["x_v"][i].rearrange("h p n -> p h n")[:, :, c * CH:(c + 1) * CH]
                         ).then_inc(s(f"x_in{c}"), 16)

        sp.wait_ge(s("prepared"), 1)
        for c in range(NC):
            load(0, c)
        counts = path_counts(sp)

        def image(i, last):
            with sp.Fori(0, 4) as r:
                for u in range(4):
                    sp.wait_ge(s(f"xt_copied{u}"), i * 4 + r + 1 + OPEN)
                    dst = xtd[ds(R + 16 * r + 4 * u, 4), :, :]
                    sp.dma_start(dst.rearrange("(m a) w c -> (a w) m c", a=2),
                                 stage[u].rearrange("p (m c) -> p m c", m=2)).then_inc(s(f"xt_out{u}"), 16)
            for u in range(4):
                sp.wait_ge(s(f"xt_out{u}"), (i + 1) * (16 * 4) + OPEN)
            sp.wait_ge(s("r_done"), (i + 1) * NC + OPEN)
            is_far, far, near = which_path(sp, i, counts)
            with sp.If(is_far):
                with sp.Fori(0, NM * NO) as g:
                    with sp.Fori(0, NB) as q:
                        sp.wait_ge(s("far_used"), (far * (NM * NO) + g) * NB + q + OPEN)
                        sp.dma_start(xt[:, 0, 0, :], xtd[ds(R + PR * q, PR), :, :]).then_inc(s("far_in"), 16)
                sp.reg_add(counts[0], counts[0], 1)
            with sp.Else():
                with sp.Fori(0, NM) as j:
                    for u in range(2):
                        sp.wait_ge(s(f"xt_used{u}"), i * NM + j + OPEN)
                        for t in range(NT):
                            src = xtd[ds(2 * PR * j + PR * u, QR), QC * t:QC * (t + 1), :]
                            sp.dma_start(xt[:, u, t, :], src).then_inc(s(f"xt_in{u}"), 16)
            for c in range(NC + 1):
                if c < NC:
                    sp.wait_ge(s("y_ready"), i * NC + c + 1 + OPEN)
                    sp.dma_start(out[i].rearrange("h p n -> p h n")[:, :, c * CH:(c + 1) * CH],
                                 x[:, :, c * CH:(c + 1) * CH]).then_inc(s(f"y_out{c}"), 16)
                if c >= 1 and not last:
                    sp.wait_ge(s(f"y_out{c - 1}"), (i + 1) * 16)
                    load(i + 1, c - 1)

        with sp.Fori(0, ni - 1) as i:
            image(i, False)
        image(ni - 1, True)
        for c in range(NC):
            sp.wait_ge(s(f"y_out{c}"), ni * 16)

    @block.gpsimd
    def _(pool):
        amax = bass.bass_isa.ReduceOp.max
        for name in OPENED:
            pool.sem_inc(s(name), OPEN)
        nc.gpsimd.memset(wo_raw, 0.0)
        nc.gpsimd.memset(dxw[:, :], 0.0)
        nc.gpsimd.memset(far_max[:, :], 0.0)
        nc.gpsimd.memset(memv[:, :], 1.0)
        nc.gpsimd.memset(zero16[:, :], 0.0)
        nc.gpsimd.memset(vhat[:, :], 0.0).then_inc(s("zeroed"), 1)
        for n in range(2):
            pool.wait_ge(s("wmax_ready"), n + 1)
            nc.gpsimd.partition_all_reduce(wall[:, n, 0:1], wmax[:, n, 0:1], P, amax).then_inc(s("wall_ready"), 1)
        with pool.Fori(0, ni) as i:
            pool.wait_ge(s("prepared"), 1)
            pool.wait_ge(s("y_ready"), i * NC + OPEN)
            stand(pool)
            for part in range(2):
                for h in range(NH):
                    v = xp[:, part, h]
                    nc.gpsimd.memset(v[:, 0:W], 0.0)
                    nc.gpsimd.memset(v[:, (PADR - 1) * W:PADR * W], 0.0).then_inc(s("border"), 1)
            pool.wait_ge(s("far_max_ready"), i + 1)
            stand(pool)
            nc.gpsimd.partition_all_reduce(far_red[:, 1:2], far_red[:, 0:1], P, amax).then_inc(s("far_all"), 1)
            pool.wait_ge(s("off_ready"), (i + 1) * NC)
            stand(pool)
            nc.gpsimd.memset(kv[:, :, 2 * HID:2 * HID + 1], 1.0).then_inc(s("v_ones"), 1)

    def gn_dve(layer, d, i):
        n_st = NC if layer == 0 else NM
        stand(nc.vector)
        for h in range(NH):
            d.inc(nc.vector.bn_aggr(mv[:, h, :], st[layer][:, h, 0:n_st, :]))
        d.wait()
        d.inc(nc.vector.tensor_copy(gst[:, 0, :], mv[:, :, 0]))
        d.inc(nc.vector.tensor_tensor(gst[:, 1, :], mv[:, :, 0], mv[:, :, 0], ALU.mult))
        d.wait()
        nc.vector.tensor_tensor(gst[:, 1, :], gst[:, 1, :], mv[:, :, 1], ALU.add).then_inc(s(f"gn_sums{layer}"), 1)
        nc.vector.wait_ge(s(f"gn_means{layer}"), i + 1)
        d.inc(nc.vector.tensor_copy(gst[:, 2:4, :], bank[0][:, 0:4].rearrange("p (a h) -> p a h", h=NH)))
        d.wait()
        d.inc(nc.vector.tensor_tensor(gst[:, 4, :], gst[:, 2, :], gst[:, 2, :], ALU.mult))
        d.wait()
        d.inc(nc.vector.tensor_tensor(gst[:, 4, :], gst[:, 3, :], gst[:, 4, :], ALU.subtract))
        d.wait()
        nc.vector.tensor_scalar(gst[:, 4, :], gst[:, 4, :], 0.0, EPS, ALU.max, ALU.add).then_inc(s(f"gn_var{layer}"), 1)
        nc.vector.wait_ge(s(f"gn_sqrt{layer}"), i + 1)
        d.inc(nc.vector.reciprocal(gst[:, 6, :], gst[:, 5, :]))
        d.wait()
        d.inc(nc.vector.tensor_tensor(gst[:, 7, :], gst[:, 6, :], gst[:, 6, :], ALU.mult))
        d.wait()
        d.inc(nc.vector.tensor_tensor(gst[:, 7, :], gst[:, 7, :], gst[:, 4, :], ALU.mult))
        d.wait()
        d.inc(nc.vector.tensor_scalar(gst[:, 7, :], gst[:, 7, :], -0.5, 1.5, ALU.mult, ALU.add))
        d.wait()
        sc = SX if layer == 0 else 1.0
        d.inc(nc.vector.scalar_tensor_tensor(gst[:, 9, :], gst[:, 6, :], sc, gst[:, 7, :], ALU.mult, ALU.mult))
        d.wait()
        d.inc(nc.vector.scalar_tensor_tensor(gst[:, 10, :], gst[:, 2, :], -1.0, gst[:, 9, :], ALU.mult, ALU.mult))
        d.wait()

    GN_STEPS = 2 + 2 + 1 + 2 + 4 + 2

    @block.vector
    def _(dve):
        d = Count(dve, s("dve_prep"))
        def scale_of(n, rows, raw, back):
            d.inc(nc.vector.memset(wmax[:, n, :], 0.0))
            d.wait()
            nc.vector.tensor_reduce(wmax[rows, n, 0:1], raw, mybir.AxisListType.XY if len(raw.shape) == 3 else X,
                                    ALU.max, apply_absolute_value=True).then_inc(s("wmax_ready"), 1)
            dve.wait_ge(s("wall_ready"), n + 1)
            d.inc(nc.vector.tensor_scalar(wall[:, n, 1:2], wall[:, n, 0:1], 1e-30, None, ALU.max))
            d.wait()
            d.inc(nc.vector.reciprocal(wall[:, n, 2:3], wall[:, n, 1:2]))
            d.inc(nc.vector.tensor_scalar(wall[:, n, 3:4], wall[:, n, 1:2], back, None, ALU.mult))
            d.wait()
            d.inc(nc.vector.tensor_scalar(wall[:, n, 2:3], wall[:, n, 2:3], SW, None, ALU.mult))
            d.wait()

        dve.wait_ge(s("wc_in"), 16)
        scale_of(0, slice(0, P), wc_raw, 1.0 / (SW * SX * SA))
        d.inc(nc.vector.tensor_scalar(wc_raw, wc_raw, wall[:, 0, 2:3], None, ALU.mult))
        d.wait()
        d.inc(nc.vector.tensor_copy(wc_hl[0], wc_raw))
        d.wait()
        nc.vector.tensor_tensor(wc_hl[1], wc_raw, wc_hl[0], ALU.subtract).then_inc(s("wc_split"), 1)
        dve.wait_ge(s("wo_in"), 16)
        scale_of(1, slice(0, P), wo_raw, 1.0 / (SW * SX))
        wo_v = wo_raw.rearrange("p (c t) -> p t c", t=KK)
        wo_hi = wo_hl[0].rearrange("p (t c) -> p t c", t=KK)
        wo_lo = wo_hl[1].rearrange("p (t c) -> p t c", t=KK)
        d.inc(nc.vector.tensor_scalar(wo_raw, wo_raw, wall[:, 1, 2:3], None, ALU.mult))
        d.wait()
        d.inc(nc.vector.tensor_copy(wo_hi, wo_v))
        d.wait()
        nc.vector.tensor_tensor(wo_lo, wo_v, wo_hi, ALU.subtract).then_inc(s("wo_split"), 1)
        dve.wait_ge(s("const_in"), 16 * N_CONST)
        for e in range(NWT):
            dve.wait_ge(s("wt_ready"), e + 1)
            nc.vector.tensor_copy(wt[:, 2 * e:2 * e + 2, :, :].rearrange("p k a c -> p (k a c)"),
                                  bank[e % 2][:, :].bitcast(f16)).then_inc(s("wt_copied"), 1)
        for e in range(NWO):
            dve.wait_ge(s("wt_ready"), NWT + e + 1)
            m = min(8, 2 * KK * NH - 8 * e)
            nc.vector.tensor_copy(wofft[:, 4 * e:4 * e + m // 2, :, :].rearrange("p k a c -> p (k a c)"),
                                  bank[(NWT + e) % 2][:, :].bitcast(f16)[:, 0:32 * m]).then_inc(s("wt_copied"), 1)
        for a in range(3):
            for h in range(NH):
                n = a * NH + h
                dve.wait_ge(s("wa_ready"), n + 1)
                nc.vector.tensor_scalar(wqkvt[:, h, a * P:(a + 1) * P], bank[2 + n % 2][:, 0:P], g1[:, h:h + 1],
                                        float(C) ** 0.5, ALU.mult, ALU.mult).then_inc(s("wa_copied"), 1)
        for h in range(NH):
            n = 6 + h
            dve.wait_ge(s("wa_ready"), n + 1)
            nc.vector.tensor_copy(woutt[:, h * P:(h + 1) * P], bank[2 + n % 2][:, 0:P]).then_inc(s("wa_copied"), 1)
        dve.wait_ge(s("wa_ready"), 9)
        dve.wait_ge(s("zeroed"), 1)
        d.inc(nc.vector.tensor_copy(memv[:, 0:HID], bank[2][0:MEM, 0:P]))
        dve.wait_ge(s("bias_rows"), 1)
        d.inc(nc.vector.tensor_copy(bias_r[:, :], bank[3][:, 0:2]))
        d.wait()
        d.inc(nc.vector.tensor_tensor(bias_r[:, 0:1], bias_r[:, 0:1], small[:, 1:2], ALU.add))
        d.inc(nc.vector.tensor_scalar(bias_r[:, 1:2], bias_r[:, 1:2], 0.5, None, ALU.mult))
        d.inc(nc.vector.tensor_scalar(boff_half[:, :], boff_all[:, :], 0.5, None, ALU.mult))
        d.wait()
        nc.vector.memset(c2[:, 7, :], 1.0).then_inc(s("prepared"), 1)

        gd = [Count(dve, s(f"dve_gn{n}")) for n in range(2)]
        rd = Count(dve, s("dve_r"))
        qd, kd, od = Count(dve, s("dve_q")), Count(dve, s("dve_k")), Count(dve, s("dve_o"))
        ocn = Count(dve, s("dve_oc"))
        counts = path_counts(dve)
        with dve.Fori(0, ni) as i:
            for c in range(NC):
                dve.wait_ge(s(f"x_in{c}"), (i + 1) * 16)
                for h in range(NH):
                    nc.vector.bn_stats(st[0][:, h, c, :], x[:, h, c * CH:(c + 1) * CH]).then_inc(s("st_ready"), 1)
            dve.wait_ge(s("st_ready"), (i + 1) * (NH * NC))
            gd[0].at(i * GN_STEPS)
            gn_dve(0, gd[0], i)
            dve.wait_ge(s("border"), (i + 1) * 4)
            stand(dve)
            def normalize(r):
                for h in range(NH):
                    if r >= 1:
                        dve.wait_ge(s("xn_lo"), i * 8 + (r - 1) * 2 + h + 1)
                    nc.vector.tensor_scalar(xn_tmp[h], x[:, h, r * 1024:(r + 1) * 1024], gst[:, 9, h:h + 1],
                                            gst[:, 10, h:h + 1], ALU.mult, ALU.add).then_inc(s("xn_ready"), 1)
                for h in range(NH):
                    dve.wait_ge(s("xn_hi"), i * 8 + r * 2 + h + 1)
                    dst = [xp[:, part, h, r * 1024 + W:(r + 1) * 1024 + W] for part in range(2)]
                    nc.vector.tensor_tensor(dst[1], xn_tmp[h], dst[0], ALU.subtract).then_inc(s("xn_lo"), 1)

            normalize(0)
            for r in range(4):
                if r + 1 < 4:
                    normalize(r + 1)
                for u in (1, 3):
                    dve.wait_ge(s(f"xt_ready{u}"), i * 4 + r + 1)
                    dve.wait_ge(s(f"xt_out{u}"), (i * 4 + r) * 16 + OPEN)
                    nc.vector.tensor_copy(stage[u], bank[u][:, :].bitcast(f16)).then_inc(s(f"xt_copied{u}"), 1)
            R_STEPS = 7
            for c in range(NC):
                rd.at((i * NC + c) * R_STEPS)
                cols = slice(c * (RC * WW), (c + 1) * (RC * WW))
                dve.wait_ge(s("r_ready"), i * NC + c + 1)
                r1 = [bank[4 + n][64:105, 0:4 * WW] for n in range(2)]
                rdv = r_d[64:105, :].rearrange("p (b n) -> p b n", b=2)
                for n in range(2):
                    rd.inc(nc.vector.tensor_scalar(rdv[:, n, :], r1[n], bias_r[64:105, 0:1], 8.0, ALU.add, ALU.min))
                rd.wait()
                nc.vector.tensor_scalar(r_d[64:105, :], r_d[64:105, :], -8.0, SX, ALU.max, ALU.mult).then_inc(s("r_read"), 1)
                dve.wait_ge(s("r_read"), i * NC + c + 1)
                rd.inc(nc.vector.tensor_reduce(far_max[64:105, c:c + 1], r_d[64:105, :], X, ALU.max,
                                               apply_absolute_value=True))
                rd.inc(nc.vector.tensor_copy(dxw[64:64 + KK, cols], r_d[64:64 + KK, :]))
                rd.wait()
                rd.inc(nc.vector.tensor_tensor(dxw[96:96 + KK, cols], r_d[64:64 + KK, :], dxw[64:64 + KK, cols],
                                               ALU.subtract))
                dve.wait_ge(s("r_act"), i * NC + c + 1)
                rd.inc(nc.vector.scalar_tensor_tensor(r_v[0:63, :], r_sig[0:63, :], 1.0, r_hat[0:63, :], ALU.add,
                                                      ALU.mult))
                rd.wait()
                rd.inc(nc.vector.tensor_copy(vhat[0:63, cols], r_v[0:63, :]))
                rd.wait()
                nc.vector.tensor_tensor(vhat[64:127, cols], r_v[0:63, :], vhat[0:63, cols],
                                        ALU.subtract).then_inc(s("r_done"), 1)
            dve.wait_ge(s("r_done"), (i + 1) * NC + OPEN)
            nc.vector.tensor_reduce(far_red[:, 0:1], far_max[:, :], X, ALU.max).then_inc(s("far_max_ready"), 1)
            dve.wait_ge(s("far_all"), i + 1)
            nc.vector.tensor_scalar(far_flag[:, :], far_red[:, 1:2], R * SX, None, ALU.is_gt).then_inc(s("far_flag_ready"), 1)

            def front(f, o):
                dve.wait_ge(s("hatx_ready"), f + 1)
                dve.wait_ge(s("hy_ready"), f + 1)
                nc.vector.tensor_tensor(a_full[o % 2], hat_x[o % 2], bank[BANK_HY[o % 2]][:, 0:GW],
                                        ALU.mult).then_inc(s("a_full"), 1)
                dve.wait_ge(s("a_hi"), f + 1)
                nc.vector.tensor_tensor(a_hl[o % 3][1], a_full[o % 2], a_hl[o % 3][0],
                                        ALU.subtract).then_inc(s("a_lo"), 1)

            def sampled_psum(o):
                b = BANK_S[o % 2]
                return [bank[b + h][:, 0:GK * P].rearrange("p (k n) -> p k n", k=GK) for h in range(NH)]

            def back(f, o):
                u, g = o % MB, o // MB
                dve.wait_ge(s("s_hi"), f + 1)
                src = sampled_psum(o)
                for h in range(NH):
                    k0, n0 = g * GK, u * P
                    ins = nc.vector.tensor_tensor(S[:, 1, h, k0:k0 + GK, n0:n0 + P], src[h],
                                                  S[:, 0, h, k0:k0 + GK, n0:n0 + P], ALU.subtract)
                ins.then_inc(s("s_lo"), 1)

            def macro(m, first, last):
                for o in range(NO):
                    if o + 2 < NO or not last:
                        front((near * NM + m) * NO + o + 2, o + 2)
                    back((i * NM + m) * NO + o, o)
                    if o == MB - 1 and not first:
                        add_conv(m - 1)

            def far_group(m, n, o):
                g = o // MB
                dve.wait_ge(s("far_spread"), n + 1)
                for k in range(GK):
                    cols = slice(k * P, (k + 1) * P)
                    for b, dst, ch in ((0, far_py, g * GK + k), (1, far_px, KK + g * GK + k)):
                        ins = nc.vector.scalar_tensor_tensor(dst[:, cols], bank[b][:, cols], boff_all[:, ch:ch + 1],
                                                             far_xy[:, b, :], ALU.add, ALU.add)
                ins.then_inc(s("far_coords"), 1)
                dve.wait_ge(s("far_hat"), n + 1)
                nc.vector.scalar_tensor_tensor(far_hx, far_m, 1.0, far_hx, ALU.add, ALU.mult).then_inc(s("far_hx_ready"), 1)
                dve.wait_ge(s("far_hx_ready"), n + 1)
                stand(dve)
                with dve.Fori(0, NB) as q:
                    t = n * NB + q
                    dve.wait_ge(s("far_hy"), t + 1)
                    dve.wait_ge(s("far_used"), t + OPEN)
                    nc.vector.tensor_tensor(far_a, far_t, far_hx, ALU.mult).then_inc(s("far_a"), 1)
                    dve.wait_ge(s("far_a"), t + 1 + OPEN)
                    nc.vector.tensor_copy(far_hl[0], far_a).then_inc(s("far_a_hi"), 1)
                    dve.wait_ge(s("far_a_hi"), t + 1)
                    nc.vector.tensor_tensor(far_hl[1], far_a, far_hl[0], ALU.subtract).then_inc(s("far_a_lo"), 1)

            def far_macro(m):
                for o in range(NO):
                    far_group(m, (far * NM + m) * NO + o, o)
                    back((i * NM + m) * NO + o, o)
                add_conv(m)

            def add_conv(m):
                dve.wait_ge(s("conv2"), i * NM + m + 1 + OPEN)
                for h in range(NH):
                    xs = x[:, h, ds(m * MP, MP)]
                    ins = nc.vector.scalar_tensor_tensor(xs, bank[BANK_O][:, h * MP:(h + 1) * MP], wall[:, 0, 3:4], xs,
                                                         ALU.mult, ALU.add)
                ins.then_inc(s("x1_ready"), 1)
                dve.wait_ge(s("x1_ready"), i * NM + m + 1 + OPEN)
                for h in range(NH):
                    ins = nc.vector.bn_stats(st[1][:, h, ds(m, 1), :], x[:, h, ds(m * MP, MP)])
                ins.then_inc(s("st1_ready"), 1)

            is_far, far, near = which_path(dve, i, counts)
            with dve.If(is_far):
                with dve.Fori(0, NM) as m:
                    far_macro(m)
                dve.reg_add(counts[0], counts[0], 1)
            with dve.Else():
                for o in range(2):
                    front(near * (NM * NO) + o, o)
                macro(0, True, False)
                with dve.Fori(1, NM - 1) as m:
                    macro(m, False, False)
                macro(NM - 1, False, True)
                add_conv(NM - 1)
                dve.reg_add(counts[1], counts[1], 1)

            dve.wait_ge(s("st1_ready"), (i + 1) * NM)
            gd[1].at(i * GN_STEPS)
            gn_dve(1, gd[1], i)

            def normalized(slot, c):
                for h in range(NH):
                    ins = nc.vector.tensor_scalar(an[slot][:, h, :], x[:, h, ds(c * CH, CH)], gst[:, 9, h:h + 1],
                                                  gst[:, 10, h:h + 1], ALU.mult, ALU.add)
                ins.then_inc(s("an_ready"), 1)

            stand(dve)
            with dve.Fori(0, NC // 2) as c:
                for u in range(2):
                    dve.wait_ge(s(f"sq_ready{u}"), i * (NC // 2) + c + 1 + OPEN)
                    nc.vector.tensor_tensor(sq[u][:, 0, :], sq[u][:, 0, :], sq[u][:, 1, :],
                                            ALU.add).then_inc(s("sq_added"), 1)
            normalized(0, 0)
            od.at(i * 4)
            dve.wait_ge(s("norm_sqrt"), i + 1)
            od.inc(nc.vector.memset(kmx, -3.0e38))
            od.inc(nc.vector.tensor_scalar(c1[:, 1, :], c1[:, 0, :], 1e-12, None, ALU.max))
            od.wait()
            nc.vector.reciprocal(c1[:, 2, :], c1[:, 1, :]).then_inc(s("rnorm"), 1)
            dve.wait_ge(s("rnorm"), i + 1)
            Q_STEPS = 4

            def wide(v):
                return v.rearrange("p (g o) -> p g o", o=1).to_broadcast([P, 16, DH])

            for n in range(NC):
                u, at = n % 2, i * NC + n
                if n + 1 < NC:
                    if n >= 1:
                        dve.wait_ge(s("qkv_tile"), i * NB + 4 * n)
                    normalized(1 - u, n + 1)
                qd.at(at * Q_STEPS)
                dve.wait_ge(s("tile_copied"), i * NB + 4 * n + 4)
                q3 = qs[u].rearrange("p (g d) -> p g d", d=DH)
                e3 = qe[u].rearrange("p (g d) -> p g d", d=DH)
                mx, sm, rs = c2[:, 3 * u, :], c2[:, 3 * u + 1, :], c2[:, 3 * u + 2, :]
                qd.inc(nc.vector.tensor_reduce(mx, q3, X, ALU.max))
                qd.wait()
                nc.vector.tensor_tensor(q3, q3, wide(mx), ALU.subtract).then_inc(s("q_shifted"), 1)
                kx = kmx.rearrange("p (t d) -> p t d", t=4)
                qd.inc(nc.vector.tensor_tensor(kx, kx, kv[:, 4 * n:4 * n + 4, 0:HID], ALU.max))
                dve.wait_ge(s("q_exp"), at + 1)
                qd.inc(nc.vector.tensor_reduce(sm, e3, X, ALU.add))
                qd.wait()
                qd.inc(nc.vector.reciprocal(rs, sm))
                qd.wait()
                nc.vector.tensor_tensor(e3, e3, wide(rs), ALU.mult).then_inc(s("q_ready"), 1)
            kd.at(i * 4)
            nc.vector.tensor_reduce(kred, kmx.rearrange("p (t d) -> p d t", t=4), X, ALU.max).then_inc(s("kred_ready"), 1)
            dve.wait_ge(s("kred_t"), i + 1)
            kd.inc(nc.vector.tensor_reduce(c2[:, 6, 0:1], bank[6][:, 0:P], X, ALU.max))
            kd.inc(nc.vector.tensor_reduce(c2[:, 6, 1:2], memk[:, :], X, ALU.max))
            kd.wait()
            kd.inc(nc.vector.tensor_tensor(c2[:, 6, 2:3], c2[:, 6, 0:1], c2[:, 6, 1:2], ALU.max))
            kd.wait()
            kd.inc(nc.vector.tensor_scalar(c2[:, 6, 3:4], c2[:, 6, 2:3], -1.0, None, ALU.mult))
            kd.wait()
            nc.vector.tensor_scalar(kdiag, ident32[:, :], c2[:, 6, 2:3], None, ALU.mult).then_inc(s("kdiag_ready"), 1)
            dve.wait_ge(s("kmb_ready"), i + 1)
            nc.vector.tensor_copy(kmb, bank[6][:, 0:P]).then_inc(s("kmb_copied"), 1)
            dve.wait_ge(s("kmb_copied"), i + 1)
            stand(dve)
            with dve.Fori(0, NC // 2) as c:
                for u in range(2):
                    dve.wait_ge(s(f"ek_ready{u}"), i * (NC // 2) + c + OPEN)
                    nc.vector.tensor_tensor(ekx[u].rearrange("p (t d) -> p t d", t=4), kv[:, ds((2 * c + u) * 4, 4), 0:HID],
                                            kmb.rearrange("p (o d) -> p o d", o=1).to_broadcast([P, 4, HID]),
                                            ALU.subtract).then_inc(s("k_shifted"), 1)
            dve.wait_ge(s("ekm_t"), i + 1)
            nc.vector.tensor_copy(ekmt[0:MEM, :], bank[6][0:MEM, 0:P]).then_inc(s("ekmt_ready"), 1)
            dve.wait_ge(s("ctx_ready"), i + 1)
            od.at(i * 4 + 2)
            od.inc(nc.vector.reciprocal(c2[:, 6, 4:5], bank[7][:, HID:HID + 1]))
            od.wait()
            od.inc(nc.vector.tensor_scalar(ctxn, bank[7][:, 0:HID], c2[:, 6, 4:5], float(DH) ** -0.5, ALU.mult, ALU.mult))
            od.wait()
            nc.vector.tensor_tensor(ctxn, ctxn, head_mask[:, :], ALU.mult).then_inc(s("ctxn_ready"), 1)
            dve.wait_ge(s("ctx_t"), i + 1)
            nc.vector.tensor_copy(ctxt, bank[6][:, 0:P]).then_inc(s("ctxt_ready"), 1)
            dve.wait_ge(s("m2_psum"), i + 1)
            nc.vector.tensor_copy(m2, bank[6][:, 0:C]).then_inc(s("m2_ready"), 1)
            O_STEPS = 2
            for n in range(NC + 2):
                if 1 <= n <= NC:
                    m, at = n - 1, i * NC + n - 1
                    cs = slice(4 * (m % 4), 4 * (m % 4) + 4)
                    ocn.at(at * O_STEPS)
                    dve.wait_ge(s("o_sqrt"), at + 1)
                    ocn.inc(nc.vector.tensor_scalar(c1[:, 4, cs], c1[:, 3, cs], 1e-12 / float(C) ** 0.5, None, ALU.max))
                    ocn.wait()
                    ocn.inc(nc.vector.reciprocal(c1[:, 5, cs], c1[:, 4, cs]))
                    ocn.wait()
                    if m >= 2:
                        dve.wait_ge(s("rb_ready"), at - 1)
                    for t in range(4):
                        ins = nc.vector.tensor_scalar(odiag[m % 2][:, t * P:(t + 1) * P], ident32[:, :],
                                                      c1[:, 5, cs.start + t:cs.start + t + 1], None, ALU.mult)
                    ins.then_inc(s("odiag_ready"), 1)
                if n >= 2:
                    m, at = n - 2, i * NC + n - 2
                    a = an[m % 3]
                    dve.wait_ge(s("rb_ready"), at + 1)
                    for h in range(NH):
                        ins = nc.vector.tensor_tensor(a[:, h, :], a[:, h, :], bank[4 + 2 * (m % 2)][:, :], ALU.mult)
                    ins.then_inc(s("o_scaled"), 1)
                    dve.wait_ge(s("o_scaled"), at + 1)
                    for h in range(NH):
                        xs = x[:, h, m * CH:(m + 1) * CH]
                        ins = nc.vector.scalar_tensor_tensor(xs, a[:, h, :], g2[:, h:h + 1], xs, ALU.mult, ALU.add)
                    ins.then_inc(s("y_ready"), 1)

    @block.scalar
    def _(act):
        act.wait_ge(s("prepared"), 1)
        act.wait_ge(s("const_in"), 16 * N_CONST)
        ra = Count(act, s("act_r"))

        counts = path_counts(act)
        with act.Fori(0, ni) as i:
            act.wait_ge(s("gn_var0"), i + 1)
            nc.scalar.activation(gst[:, 5, :], gst[:, 4, :], ACT.Sqrt).then_inc(s("gn_sqrt0"), 1)
            act.wait_ge(s("border"), (i + 1) * 4)
            stand(act)
            def high_part(r):
                for h in range(NH):
                    act.wait_ge(s("xn_ready"), i * 8 + r * 2 + h + 1)
                    nc.scalar.activation(xp[:, 0, h, r * 1024 + W:(r + 1) * 1024 + W], xn_tmp[h],
                                         ACT.Copy).then_inc(s("xn_hi"), 1)

            high_part(0)
            for r in range(4):
                if r + 1 < 4:
                    high_part(r + 1)
                for u in (0, 2):
                    act.wait_ge(s(f"xt_ready{u}"), i * 4 + r + 1)
                    act.wait_ge(s(f"xt_out{u}"), (i * 4 + r) * 16 + OPEN)
                    nc.scalar.activation(stage[u], bank[u][:, :].bitcast(f16), ACT.Copy).then_inc(s(f"xt_copied{u}"), 1)
            for c in range(NC + 1):
                if c < NC:
                    act.wait_ge(s("off_ready"), i * NC + c + 1)
                    nc.scalar.activation(offs[:, c * CH:(c + 1) * CH], bank[2 + c % 2][:, :], ACT.Copy,
                                         scale=wall[:, 1, 3:4]).then_inc(s("off_copied"), 1)
                if c >= 1:
                    at = i * NC + c - 1
                    ra.at(at * 4)
                    act.wait_ge(s("r_ready"), at + 1)
                    act.wait_ge(s("r_done"), at + OPEN)
                    av = r_abs[0:63, :].rearrange("p (b n) -> p b n", b=2)
                    sv = r_sig[0:63, :].rearrange("p (b n) -> p b n", b=2)
                    for n in range(2):
                        ra.inc(nc.scalar.activation(sv[:, n, :], bank[6 + n][0:63, 0:4 * WW], ACT.Tanh,
                                                    bias=bias_r[0:63, 1:2], scale=0.5))
                    for n in range(2):
                        ra.inc(nc.scalar.activation(av[:, n, :], bank[4 + n][0:63, 0:4 * WW], ACT.Abs,
                                                    bias=bias_r[0:63, 0:1]))
                    ra.wait()
                    nc.scalar.activation(r_hat[0:63, :], r_abs[0:63, :], ACT.Relu, bias=SA / 2,
                                         scale=-SA / 2).then_inc(s("r_act"), 1)

            def front(f, o):
                act.wait_ge(s("hx_ready"), f + 1)
                nc.scalar.activation(t_abs[0], bank[BANK_HX][:, 0:GW], ACT.Abs, bias=small[:, 0:1],
                                     scale=1.0 / SX).then_inc(s("hx_read"), 1)
                act.wait_ge(s("hx_read"), f + 1 + OPEN)
                nc.scalar.activation(hat_x[o % 2], t_abs[0], ACT.Relu, bias=1.0, scale=-1.0).then_inc(s("hatx_ready"), 1)
                act.wait_ge(s("a_full"), f + 1)
                nc.scalar.activation(a_hl[o % 3][0], a_full[o % 2], ACT.Copy).then_inc(s("a_hi"), 1)

            def back(f, o):
                u, g = o % MB, o // MB
                act.wait_ge(s("sampled"), f + 1)
                for h in range(NH):
                    src = bank[BANK_S[o % 2] + h][:, 0:GK * P].rearrange("p (k n) -> p k n", k=GK)
                    ins = nc.scalar.activation(S[:, 0, h, g * GK:(g + 1) * GK, u * P:(u + 1) * P], src, ACT.Copy)
                ins.then_inc(s("s_hi"), 1)

            def far_group(m, n, o):
                g = o // MB
                act.wait_ge(s("far_spread"), n + 1)
                for k in range(GK):
                    cols = slice(k * P, (k + 1) * P)
                    ch = 2 * KK + g * GK + k
                    nc.scalar.activation(far_m[:, cols], bank[2][:, cols], ACT.Tanh, bias=boff_half[:, ch:ch + 1], scale=0.5)
                act.wait_ge(s("far_coords"), n + 1)
                nc.scalar.activation(far_px, far_px, ACT.Abs).then_inc(s("far_px_abs"), 1)
                act.wait_ge(s("far_px_abs"), n + 1)
                nc.scalar.activation(far_hx, far_px, ACT.Relu, bias=SA / 2, scale=-SA / 2).then_inc(s("far_hat"), 1)
                with act.Fori(0, NB) as q:
                    t = n * NB + q
                    act.wait_ge(s("far_a"), t + OPEN)
                    nc.scalar.activation(far_t, far_py, ACT.Abs, bias=far_rows[:, ds(MB * m + o % MB + NB - 1 - q, 1)]
                                         ).then_inc(s("far_py_abs"), 1)
                    act.wait_ge(s("far_py_abs"), t + 1)
                    nc.scalar.activation(far_t, far_t, ACT.Relu, bias=1.0, scale=-1.0).then_inc(s("far_hy"), 1)

            def far_macro(m):
                for o in range(NO):
                    far_group(m, (far * NM + m) * NO + o, o)
                    if o % MB == 0:
                        act.wait_ge(s(f"conv{o // MB}"), i * NM + m + OPEN)
                    back((i * NM + m) * NO + o, o)

            def macro(m, first, last):
                base = (i * NM + m) * NO
                for o in range(NO):
                    if o + 2 < NO or not last:
                        if o + 2 >= 3:
                            act.wait_ge(s("sampled"), base + o)
                        front((near * NM + m) * NO + o + 2, o + 2)
                    if o % MB == 0:
                        act.wait_ge(s(f"conv{o // MB}"), i * NM + m + OPEN)
                    back(base + o, o)

            act.wait_ge(s("r_done"), (i + 1) * NC + OPEN)
            is_far, far, near = which_path(act, i, counts)
            with act.If(is_far):
                with act.Fori(0, NM) as m:
                    far_macro(m)
                act.reg_add(counts[0], counts[0], 1)
            with act.Else():
                for o in range(2):
                    front(near * (NM * NO) + o, o)
                macro(0, True, False)
                with act.Fori(1, NM - 1) as m:
                    macro(m, False, False)
                macro(NM - 1, False, True)
                act.reg_add(counts[1], counts[1], 1)

            act.wait_ge(s("gn_var1"), i + 1)
            nc.scalar.activation(gst[:, 5, :], gst[:, 4, :], ACT.Sqrt).then_inc(s("gn_sqrt1"), 1)
            act.wait_ge(s("dve_gn1"), (i + 1) * GN_STEPS)
            stand(act)
            with act.Fori(0, NC // 2) as c:
                for u in range(2):
                    act.wait_ge(s(f"sq_used{u}"), i * (NC // 2) + c + OPEN)
                    for h in range(NH):
                        ins = nc.scalar.activation(sq[u][:, h, :], x[:, h, ds((2 * c + u) * CH, CH)], ACT.Square,
                                                   bias=gst[:, 10, h:h + 1], scale=gst[:, 9, h:h + 1])
                    ins.then_inc(s(f"sq_ready{u}"), 1)
            act.wait_ge(s("norm_sums"), i + 1)
            nc.scalar.activation(c1[:, 0, :], bank[2][:, 0:NB], ACT.Sqrt).then_inc(s("norm_sqrt"), 1)
            act.wait_ge(s("rnorm"), i + 1)

            def q_back(n):
                act.wait_ge(s("q_t"), i * NC + n + 1)
                nc.scalar.activation(q_soft[:, n * CH:(n + 1) * CH], bank[4 + n % 2][:, :],
                                     ACT.Copy).then_inc(s("q_t_copied"), 1)

            for n in range(NC):
                u = n % 2
                if n >= 2:
                    act.wait_ge(s("q_t"), i * NC + n - 1)
                for t in range(4):
                    ti = 4 * n + t
                    act.wait_ge(s("qkv_tile"), i * NB + ti + 1)
                    nc.scalar.activation(qs[u][:, t * HID:(t + 1) * HID], bank[t][:, 0:HID], ACT.Copy,
                                         scale=c1[:, 2, ti:ti + 1])
                    nc.scalar.activation(kv[:, ti, 0:2 * HID], bank[t][:, HID:3 * HID], ACT.Copy,
                                         scale=c1[:, 2, ti:ti + 1]).then_inc(s("tile_copied"), 1)
                if n >= 1:
                    q_back(n - 1)
                act.wait_ge(s("q_shifted"), i * NC + n + 1)
                nc.scalar.activation(qe[u], qs[u], ACT.Exp).then_inc(s("q_exp"), 1)
            q_back(NC - 1)
            act.wait_ge(s("kdiag_ready"), i + 1)
            nc.scalar.activation(ekm[:, 0:MEM], memk[:, :], ACT.Exp, bias=c2[:, 6, 3:4]).then_inc(s("ekm_ready"), 1)
            with act.Fori(0, NC // 2) as c:
                for u in range(2):
                    act.wait_ge(s("k_shifted"), i * NC + 2 * c + u + 1)
                    act.wait_ge(s(f"ctx_done{u}"), i * (NC // 2) + c + OPEN)
                    nc.scalar.activation(ek[u], ekx[u], ACT.Exp).then_inc(s(f"ek_ready{u}"), 1)
            for n in range(NC + 1):
                if n < NC:
                    at = i * NC + n
                    act.wait_ge(s("o_psum"), at + 1)
                    if n >= 3:
                        act.wait_ge(s("y_ready"), at - 2 + OPEN)
                    for h in range(NH):
                        ins = nc.scalar.activation(an[n % 3][:, h, :], bank[2 * (n % 2) + h][:, :], ACT.Identity,
                                                   bias=bout[:, h:h + 1])
                    ins.then_inc(s("o_copied"), 1)
                    if n >= 2:
                        act.wait_ge(s("osum_ready"), at - 1)
                    act.wait_ge(s("o_copied"), at + 1)
                    nc.scalar.activation(sq[n % 2], an[n % 3], ACT.Square).then_inc(s("osq_ready"), 1)
                if n >= 1:
                    m, at = n - 1, i * NC + n - 1
                    act.wait_ge(s("osum_ready"), at + 1)
                    nc.scalar.activation(c1[:, 3, 4 * (m % 4):4 * (m % 4) + 4], bank[5 + 2 * (m % 2)][:, 0:4], ACT.Sqrt,
                                         scale=1.0 / C).then_inc(s("o_sqrt"), 1)

    @block.tensor
    def _(pe):
        mm = nc.tensor.matmul
        pe.wait_ge(s("const_in"), 16 * N_CONST)
        pe.wait_ge(s("wc_split"), 1)
        for e in range(NWT):
            if e >= 2:
                pe.wait_ge(s("wt_copied"), e - 1)
            b = bank[e % 2][:, :].bitcast(f16)
            for n in range(8):
                k, half, part, oh = (2 * e + n // 4) // NH, (2 * e + n // 4) % NH, n // 2 % 2, n % 2
                c0 = k * C + half * P
                ins = nc.tensor.transpose(b[:, n * P:(n + 1) * P], wc_hl[part][:, oh, c0:c0 + P], ident16[:, :])
            ins.then_inc(s("wt_ready"), 1)
        pe.wait_ge(s("wo_split"), 1)
        for e in range(NWO):
            pe.wait_ge(s("wt_copied"), NWT + e - 1)
            b = bank[(NWT + e) % 2][:, :].bitcast(f16)
            for n in range(min(8, 2 * KK * NH - 8 * e)):
                kh, part = (8 * e + n) // 2, n % 2
                tap, half = kh // NH, kh % NH
                c0 = tap * C + half * P
                ins = nc.tensor.transpose(b[:, n * 32:(n + 1) * 32], wo_hl[part][0:32, c0:c0 + P], ident16[0:32, 0:32])
            ins.then_inc(s("wt_ready"), 1)
        pe.wait_ge(s("wa_in"), 32)
        for n in range(9):
            if n >= 2:
                pe.wait_ge(s("wa_copied"), n - 1)
            if n < 6:
                src = wq_raw[:, n // NH, (n % NH) * P:(n % NH + 1) * P]
            elif n < 8:
                src = wu_raw[:, n - 6, :]
            else:
                src = memv_raw[:, :]
            nc.tensor.transpose(bank[2 + n % 2][0:src.shape[1], 0:P], src, ident32[:, :]).then_inc(s("wa_ready"), 1)
        pe.wait_ge(s("wa_copied"), 8)
        mm(bank[3][:, 0:1], spread[0:27, 0, :], boff[:, :], start=True, stop=True)
        mm(bank[3][:, 1:2], spread[0:27, 1, :], boff[:, :], start=True, stop=True).then_inc(s("bias_rows"), 1)

        counts = path_counts(pe)
        PASSES = [(0, 0), (0, 1), (1, 0)]

        with pe.Fori(0, ni) as i:
            pe.wait_ge(s("gn_sums0"), i + 1)
            mm(bank[0][:, 0:4], group_mean[:, :], gst[:, 0:2, :].rearrange("p a h -> p (a h)"), start=True,
               stop=True).then_inc(s("gn_means0"), 1)
            with pe.Fori(0, 4) as r:
                pe.wait_ge(s("xn_lo"), i * 8 + r * 2 + 2)
                for u in range(4):
                    pe.wait_ge(s(f"xt_copied{u}"), i * 4 + r + OPEN)
                    b = bank[u][:, :].bitcast(f16)
                    for n in range(8):
                        m, part, half = n // 4, n // 2 % 2, n % 2
                        src = xp[:, part, half, ds((16 * r + 4 * u + 2 * m + 1) * W, P)]
                        ins = nc.tensor.transpose(b[:, n * P:(n + 1) * P], src, ident16[:, :])
                    ins.then_inc(s(f"xt_ready{u}"), 1)
            def offsets(c):
                if c >= 2:
                    pe.wait_ge(s("off_copied"), i * NC + c - 1)
                else:
                    pe.wait_ge(s(f"xt_copied{2 + c}"), (i + 1) * 4 + OPEN)
                for r in range(-(-KK * NH // 4)):
                    for a, b in PASSES:
                        for j in range(4):
                            n = 4 * r + j
                            if n < KK * NH:
                                tap, half = n // NH, n % NH
                                y0, dx = c * RC + tap // 3, tap % 3 - 1
                                a0, a1 = max(0, -dx), W - max(0, dx)
                                dst = bank[2 + c % 2][32 * j:32 * j + 32, :].rearrange("p (r w) -> p r w", w=W)
                                src = xp[:, b, half, y0 * W:(y0 + RC) * W].rearrange("p (r w) -> p r w", w=W)
                                ins = mm(dst[:, :, a0:a1], wofft[:, n, a, :], src[:, :, a0 + dx:a1 + dx], start=n < 4 and (a, b) == (0, 0),
                                         stop=n + 4 >= KK * NH and (a, b) == PASSES[-1], skip_group_check=True)
                ins.then_inc(s("off_ready"), 1)
            def spread_out(c):
                pe.wait_ge(s("off_copied"), i * NC + c + 1)
                if c >= 1:
                    pe.wait_ge(s("r_read"), i * NC + c)
                    pe.wait_ge(s("r_act"), i * NC + c)
                for n in range(4):
                    for t in range(NT):
                        a, e = WIN[t]
                        p0 = (c * RC + 4 * (n % 2)) * W
                        src = offs[:, p0:p0 + 4 * W].rearrange("p (r w) -> p r w", w=W)[:, :, a:e]
                        dst = bank[4 + n][:, 0:4 * WW].rearrange("p (r w) -> p r w", w=WW)[:, :, WOFF[t]:WOFF[t] + e - a]
                        ins = mm(dst, spread[:, n // 2, :], src, start=True, stop=True)
                ins.then_inc(s("r_ready"), 1)

            for c in range(NC + 1):
                if c < NC:
                    offsets(c)
                if c >= 1:
                    spread_out(c - 1)

            def front(f, m, o):
                u, g = o % MB, (o // MB) % NG
                row = PR * (MB * m + u) if o < NO else PR * (MB * m + MB + u)
                pe.wait_ge(s("hx_read"), f + OPEN)
                for k in range(GK):
                    ins = mm(bank[BANK_HX][:, k * PR * WW:(k + 1) * PR * WW], pick_x[:, g * GK + k, :],
                             dxw[:, ds(row * WW, PR * WW)], start=True, stop=True)
                ins.then_inc(s("hx_ready"), 1)
                if not isinstance(o, int) or o >= 2:
                    pe.wait_ge(s("a_full"), f - 1)
                for k in range(GK):
                    for y in range(PR):
                        n = k * PR + y
                        ins = mm(bank[BANK_HY[o % 2]][:, n * WW:(n + 1) * WW], pick_y[:, g * GK + k, y, :],
                                 vhat[:, ds((row + y) * WW, WW)], start=True, stop=True)
                ins.then_inc(s("hy_ready"), 1)

            def sample(f, Gm, G, o):
                u, g = o % MB, o // MB
                pe.wait_ge(s("a_lo"), f + 1)
                pe.wait_ge(s("s_lo"), G * NO + max(0, o - 1) + OPEN)
                if g == 0:
                    pe.wait_ge(s(f"xt_in{u}"), (Gm + 1) * (16 * NT))
                for h in range(NH):
                    dst = bank[BANK_S[o % 2] + h][:, 0:GK * P].rearrange("p (k n) -> p k n", n=W)
                    for t in range(NT):
                        a0, a1 = WIN[t]
                        for a, b in PASSES:
                            src = a_hl[o % 3][b].rearrange("p (k n) -> p k n", n=WW)[:, :, WOFF[t]:WOFF[t] + a1 - a0]
                            ins = mm(dst[:, :, a0:a1], xt[:, u, t, a * C + h * P:a * C + (h + 1) * P], src,
                                     start=t == 0 and (a, b) == (0, 0), stop=t == NT - 1 and (a, b) == PASSES[-1],
                                     skip_group_check=True)
                ins.then_inc(s("sampled"), 1)

            def conv(G, g, oh):
                if oh == 0:
                    pe.wait_ge(s("s_lo"), G * NO + MB * (g + 1) + OPEN)
                    if g == 0:
                        pe.wait_ge(s("x1_ready"), G + OPEN)
                for k in range(g * GK, (g + 1) * GK):
                    for half in range(NH):
                        for a, b in PASSES:
                            first = k == 0 and half == 0 and (a, b) == (0, 0)
                            final = k == KK - 1 and half == NH - 1 and (a, b) == PASSES[-1]
                            ins = mm(bank[BANK_O][:, oh * MP:(oh + 1) * MP], wt[:, k * NH + half, a, oh * P:(oh + 1) * P],
                                     S[:, b, half, k, :], start=first and oh == 0, stop=final, skip_group_check=True)
                            if g == NG - 2 and (k, half, a, b) == (g * GK, 0, 0, 0):
                                ins.then_inc(s(f"xt_used{oh}"), 1)
                if oh == 1:
                    ins.then_inc(s(f"conv{g}"), 1)

            def macro(m, first, last):
                G, Gm = i * NM + m, near * NM + m
                for o in range(NO):
                    if o + 2 < NO or not last:
                        front(Gm * NO + o + 2, m, o + 2)
                    sample(Gm * NO + o, Gm, G, o)
                    if o >= MB:
                        conv(G, o // MB - 1, o % MB)
                    elif not first:
                        conv(G - 1, NG - 1, o)

            pe.wait_ge(s("r_done"), (i + 1) * NC + OPEN)
            def far_group(m, n, G, o):
                u, g = o % MB, o // MB
                for k in range(GK):
                    for b in range(3):
                        ch = b * KK + g * GK + k
                        ins = mm(bank[b][:, k * P:(k + 1) * P], of_channel[:, ch:ch + 1].to_broadcast([P, P]),
                                 offs[:, ds((MB * m + u) * P, P)], start=True, stop=True)
                ins.then_inc(s("far_spread"), 1)
                pe.wait_ge(s("s_lo"), G * NO + max(0, o - 1) + OPEN)
                dst = [bank[BANK_S[o % 2] + h][:, 0:GK * P] for h in range(NH)]
                some = pick_y[:, 0:2, :, :].rearrange("p a b c -> p (a b c)")[:, 0:GK * P]
                for h in range(NH):
                    mm(dst[h], zero16[:, :], some, start=True, stop=False, skip_group_check=True)
                with pe.Fori(0, NB) as q:
                    t = n * NB + q
                    pe.wait_ge(s("far_in"), (t + 1) * 16)
                    pe.wait_ge(s("far_a_lo"), t + 1)
                    for h in range(NH):
                        for a, b in PASSES:
                            ins = mm(dst[h], xt[:, 0, 0, a * C + h * P:a * C + (h + 1) * P], far_hl[b], start=False,
                                     stop=False, skip_group_check=True)
                    ins.then_inc(s("far_used"), 1)
                for h in range(NH):
                    ins = mm(dst[h], zero16[:, :], some, start=False, stop=True, skip_group_check=True)
                ins.then_inc(s("sampled"), 1)

            def far_macro(m):
                G = i * NM + m
                for o in range(NO):
                    far_group(m, (far * NM + m) * NO + o, G, o)
                for g in range(NG):
                    for oh in range(2):
                        conv(G, g, oh)

            is_far, far, near = which_path(pe, i, counts)
            with pe.If(is_far):
                with pe.Fori(0, NM) as m:
                    far_macro(m)
                pe.reg_add(counts[0], counts[0], 1)
            with pe.Else():
                for o in range(2):
                    front(near * (NM * NO) + o, 0, o)
                macro(0, True, False)
                with pe.Fori(1, NM - 1) as m:
                    macro(m, False, False)
                macro(NM - 1, False, True)
                for oh in range(2):
                    conv(i * NM + NM - 1, NG - 1, oh)
                pe.reg_add(counts[1], counts[1], 1)

            pe.wait_ge(s("gn_sums1"), i + 1)
            mm(bank[0][:, 0:4], group_mean[:, :], gst[:, 0:2, :].rearrange("p a h -> p (a h)"), start=True,
               stop=True).then_inc(s("gn_means1"), 1)
            with pe.Fori(0, NC // 2) as c:
                for u in range(2):
                    pe.wait_ge(s("sq_added"), i * NC + 2 * c + u + 1)
                    for t in range(4):
                        ins = mm(bank[2][:, ds((2 * c + u) * 4 + t, 1)], sq[u][:, 0, t * P:(t + 1) * P],
                                 ones32[:, 0:1], start=True, stop=True)
                    ins.then_inc(s(f"sq_used{u}"), 1)
            pe.wait_ge(s("gn_sqrt1"), i + 1)
            mm(bank[2][:, NB:NB + 1], ones32[:, :], ones32[:, 0:1], start=True, stop=True).then_inc(s("norm_sums"), 1)
            pe.wait_ge(s("norm_sqrt"), i + 1)
            stand(pe)

            def q_transposes(n):
                pe.wait_ge(s("q_ready"), i * NC + n + 1)
                if n >= 2:
                    pe.wait_ge(s("q_t_copied"), i * NC + n - 1)
                for t in range(4):
                    ins = nc.tensor.transpose(bank[4 + n % 2][:, t * P:(t + 1) * P], qe[n % 2][:, t * P:(t + 1) * P],
                                              ident32[:, :])
                ins.then_inc(s("q_t"), 1)

            for n in range(NC):
                pe.wait_ge(s("an_ready"), i * NC + n + 1)
                for t in range(4):
                    if n >= 1:
                        pe.wait_ge(s("tile_copied"), i * NB + 4 * (n - 1) + t + 1)
                    for h in range(NH):
                        ins = mm(bank[t][:, 0:3 * HID], an[n % 2][:, h, t * P:(t + 1) * P], wqkvt[:, h, :],
                                 start=h == 0, stop=h == NH - 1)
                    ins.then_inc(s("qkv_tile"), 1)
                if n >= 1:
                    q_transposes(n - 1)
            q_transposes(NC - 1)
            pe.wait_ge(s("kred_ready"), i + 1)
            nc.tensor.transpose(bank[6][:, 0:P], kred, ident32[:, :]).then_inc(s("kred_t"), 1)
            pe.wait_ge(s("kdiag_ready"), i + 1)
            mm(bank[6][:, 0:P], ones32[:, :], kdiag, start=True, stop=True).then_inc(s("kmb_ready"), 1)
            pe.wait_ge(s("ekm_ready"), i + 1)
            pe.wait_ge(s("kmb_copied"), i + 1)
            nc.tensor.transpose(bank[6][0:MEM, 0:P], ekm[:, 0:MEM], ident32[:, :]).then_inc(s("ekm_t"), 1)
            def context(u, tiles, start):
                for t in range(4):
                    ins = mm(bank[7][:, 0:HID + 1], ek[u][:, t * P:(t + 1) * P], tiles(t), start=start and t == 0,
                             stop=False, skip_group_check=True)
                ins.then_inc(s(f"ctx_done{u}"), 1)
            pe.wait_ge(s("v_ones"), i + 1)
            def vtile(ti):
                return kv[:, ds(ti, 1), HID:2 * HID + 1].rearrange("p t e -> p (t e)")
            for u in range(2):
                pe.wait_ge(s(f"ek_ready{u}"), i * (NC // 2) + 1 + OPEN)
                context(u, lambda t, u=u: vtile(4 * u + t), u == 0)
            with pe.Fori(1, NC // 2) as c:
                for u in range(2):
                    pe.wait_ge(s(f"ek_ready{u}"), i * (NC // 2) + c + 1 + OPEN)
                    context(u, lambda t, u=u: vtile((2 * c + u) * 4 + t), False)
            pe.wait_ge(s("ekmt_ready"), i + 1)
            mm(bank[7][:, 0:HID + 1], ekmt[0:MEM, :], memv[:, :], start=False, stop=True,
               skip_group_check=True).then_inc(s("ctx_ready"), 1)
            pe.wait_ge(s("ctxn_ready"), i + 1)
            nc.tensor.transpose(bank[6][:, 0:P], ctxn, ident32[:, :]).then_inc(s("ctx_t"), 1)
            pe.wait_ge(s("ctxt_ready"), i + 1)
            mm(bank[6][:, 0:C], ctxt, woutt[:, :], start=True, stop=True).then_inc(s("m2_psum"), 1)
            pe.wait_ge(s("m2_ready"), i + 1)
            pe.wait_ge(s("q_t_copied"), (i + 1) * NC)
            pe.wait_ge(s("tile_copied"), (i + 1) * NB)
            for n in range(NC + 2):
                if n < NC:
                    at = i * NC + n
                    if n >= 2:
                        pe.wait_ge(s("o_copied"), at - 1)
                    for h in range(NH):
                        ins = mm(bank[2 * (n % 2) + h][:, :], m2[:, h * P:(h + 1) * P], q_soft[:, n * CH:(n + 1) * CH],
                                 start=True, stop=True)
                    ins.then_inc(s("o_psum"), 1)
                if 1 <= n <= NC:
                    m, at = n - 1, i * NC + n - 1
                    pe.wait_ge(s("osq_ready"), at + 1)
                    if m >= 2:
                        pe.wait_ge(s("o_sqrt"), at - 1)
                    for t in range(4):
                        for h in range(NH):
                            ins = mm(bank[5 + 2 * (m % 2)][:, t:t + 1], sq[m % 2][:, h, t * P:(t + 1) * P],
                                     ones32[:, 0:1], start=h == 0, stop=h == NH - 1)
                    ins.then_inc(s("osum_ready"), 1)
                if n >= 2:
                    m, at = n - 2, i * NC + n - 2
                    pe.wait_ge(s("odiag_ready"), at + 1)
                    if m >= 2:
                        pe.wait_ge(s("o_scaled"), at - 1)
                    mm(bank[4 + 2 * (m % 2)][:, :], ones32[:, :], odiag[m % 2], start=True,
                       stop=True).then_inc(s("rb_ready"), 1)


_INS = ["x", "L0_conv_w_off", "L0_conv_b_off", "L0_conv_w_conv", "L1_conv_g1", "L1_conv_mem_kv", "L1_conv_w_qkv",
        "L1_conv_w_out", "L1_conv_b_out", "L1_conv_g2"]


def build_program(nc, shapes, ni):
    dram = {}
    for name, (shape, dt) in shapes.items():
        dram[name] = nc.dram_tensor(f"in_{name}_dram", shape, dt, kind="ExternalInput").ap()
    dram["x_v"] = dram["x"].rearrange("n (h p) r w -> n h p (r w)", p=P)
    y = nc.dram_tensor("out_0_dram", (ni, C, H, W), mybir.dt.float32, kind="ExternalOutput").ap()
    with ExitStack() as ctx:
        deform_attention(nc, ctx, ni, dram, y.rearrange("n (h p) r w -> n h p (r w)", p=P))


def kernel(**inputs):
    import concourse.bacc as _bacc
    from concourse import mybir as _mybir
    from concourse.bass_utils import run_bass_kernel_spmd as _run

    nc = _bacc.Bacc("TRN2", target_bir_lowering=False, num_devices=1)
    arrays, shapes = {}, {}
    for name, a in [(n, inputs[n]) for n in _INS] + list(tables().items()):
        a = np.ascontiguousarray(a)
        arrays[f"in_{name}_dram"] = a
        shapes[name] = (a.shape, _mybir.dt.from_np(a.dtype))
    ni = inputs["x"].shape[0]
    build_program(nc, shapes, ni)
    r = _run(nc, [arrays], core_ids=[0])
    return r.results[0]["out_0_dram"]
```
